# Optimizing a Trainium2 kernel written in Bass

```python
import numpy as np
import jax
import jax.numpy as jnp

def _softmax(x, axis=-1):
    return jax.nn.softmax(x, axis=axis)

def _gelu(x):
    return jax.nn.gelu(x, approximate=True)

def _silu(x):
    return jax.nn.silu(x)

def _sigmoid(x):
    return jax.nn.sigmoid(x)

def _layernorm(x, axis=-1, eps=1e-05):
    m = jnp.mean(x, axis=axis, keepdims=True)
    v = jnp.var(x, axis=axis, keepdims=True)
    return (x - m) / jnp.sqrt(v + eps)

def _scatter_add(tgt, idx, src, axis=0):
    return tgt.at[idx].add(src)

def _segment_sum(src, seg, n):
    return jax.ops.segment_sum(src, seg, n)
kernel_name = 'mk_prb_d1_jaxref_r8_c16014'

def setup_inputs(seed: int=0):
    np.random.seed(seed)
    _w = jnp.asarray

    def _L0_attn_setup():
        import jax, jax.numpy as jnp
        import numpy as np
        B, T, C = (64, 32, 128)
        N_HEAD, HEAD_SIZE, KV_RANK = (16, 64, 128)
        BLOCK_SIZE = 32
        key = jax.random.key(seed)
        ks = jax.random.split(key, 5)
        HD = N_HEAD * HEAD_SIZE

        def init(k, shape):
            fan_in = shape[0]
            bound = 1.0 / np.sqrt(fan_in)
            return jax.random.uniform(k, shape, jnp.float32, -bound, bound)
        return {'x': jax.random.normal(ks[0], (B, T, C), jnp.float32), 'w_kv_down': init(ks[1], (C, KV_RANK)), 'w_kv_up': init(ks[2], (KV_RANK, 2 * HD)), 'w_q': init(ks[3], (C, HD)), 'w_out': init(ks[4], (HD, C))}
    _L0_attn_in = _L0_attn_setup()

    def _L0_ffn_setup():
        import jax, jax.numpy as jnp
        import numpy as np
        DIM = 128
        DEPTH = 6
        HEADS = 16
        DIM_HEAD = 64
        WINDOW = 32
        INNER = HEADS * DIM_HEAD
        DIM_INNER = int(DIM * 4 * 2 / 3)
        QK_SCALE = 8.0

        def shift_tokens(t):
            a, s = jnp.split(t, 2, -1)
            s = jnp.pad(s, ((0, 0), (1, 0), (0, 0)))[:, :-1]
            return jnp.concatenate([a, s], -1)

        def l2norm(t):
            return t / jnp.maximum(jnp.linalg.norm(t, axis=-1, keepdims=True), 1e-12)

        def rotate_half(x):
            x1, x2 = jnp.split(x, 2, -1)
            return jnp.concatenate([-x2, x1], -1)

        def rotary_tables(n):
            half = jnp.arange(0, DIM_HEAD, 2, dtype=jnp.float32)
            inv_freq = 1.0 / 10000.0 ** (half / DIM_HEAD)
            t = jnp.arange(n, dtype=jnp.float32)
            freqs = t[:, None] * inv_freq[None, :]
            freqs = jnp.concatenate([freqs, freqs], -1)
            base_scale = (half + 0.4 * DIM_HEAD) / (1.4 * DIM_HEAD)
            power = (t - n // 2) / (WINDOW // 2)
            scale = base_scale[None, :] ** power[:, None]
            scale = jnp.concatenate([scale, scale], -1)
            return (freqs, scale)

        def local_attention(q, k, v):
            b, h, n, d = q.shape
            w = WINDOW
            nw = n // w
            bq = q.reshape(b, h, nw, w, d)
            bk = k.reshape(b, h, nw, w, d)
            bv = v.reshape(b, h, nw, w, d)

            def look(t):
                p = jnp.pad(t, ((0, 0), (0, 0), (1, 0), (0, 0), (0, 0)))
                return jnp.concatenate([p[:, :, :nw], p[:, :, 1:]], axis=3)
            bk2, bv2 = (look(bk), look(bv))
            seq = jnp.arange(n).reshape(nw, w)
            seq_p = jnp.pad(seq, ((1, 0), (0, 0)), constant_values=-1)
            jt = jnp.concatenate([seq_p[:nw], seq_p[1:]], axis=1)
            it = seq[:, :, None]
            jb = jt[:, None, :]
            mask = (it < jb) | (it > jb + w) | (jb == -1)
            sim = jnp.einsum('bhwie,bhwje->bhwij', bq, bk2) * QK_SCALE
            sim = jnp.where(mask, -jnp.finfo(sim.dtype).max, sim)
            attn = jax.nn.softmax(sim, -1)
            out = jnp.einsum('bhwij,bhwje->bhwie', attn, bv2)
            return out.reshape(b, h, n, d)

        def attn_layer(x, Wqkv, qs, ksc, Wo):
            b, n, _ = x.shape
            qkv = x @ Wqkv
            q, k, v = jnp.split(qkv, 3, -1)
            sh = lambda t: t.reshape(b, n, HEADS, DIM_HEAD).transpose(0, 2, 1, 3)
            q, k, v = (sh(q), sh(k), sh(v))
            q = l2norm(q) * qs
            k = l2norm(k) * ksc
            freqs, scale = rotary_tables(n)
            cos, sin = (jnp.cos(freqs), jnp.sin(freqs))
            q = q * cos * scale + rotate_half(q) * sin * scale
            inv = 1.0 / scale
            k = k * cos * inv + rotate_half(k) * sin * inv
            out = local_attention(q, k, v)
            out = out.transpose(0, 2, 1, 3).reshape(b, n, INNER)
            return out @ Wo

        def ffn_layer(x, g, bln, W1, b1, W2, b2):
            mu = x.mean(-1, keepdims=True)
            var = ((x - mu) ** 2).mean(-1, keepdims=True)
            xn = (x - mu) / jnp.sqrt(var + 1e-05) * g + bln
            hg = xn @ W1 + b1
            a, gate = jnp.split(hg, 2, -1)
            return a * jax.nn.gelu(gate, approximate=False) @ W2 + b2
        key = jax.random.key(seed)
        ks = jax.random.split(key, 8)
        B, N = (2, 256)
        init = lambda k, shape: jax.random.normal(k, shape, jnp.float32) * 0.02
        return {'x': jax.random.normal(ks[0], (B, N, DIM), jnp.float32), 'Wqkv': init(ks[1], (DEPTH, DIM, 3 * INNER)), 'q_scale': jnp.ones((DEPTH, DIM_HEAD), jnp.float32), 'k_scale': jnp.ones((DEPTH, DIM_HEAD), jnp.float32), 'Wo': init(ks[2], (DEPTH, INNER, DIM)), 'ln_g': jnp.ones((DEPTH, DIM), jnp.float32), 'ln_b': jnp.zeros((DEPTH, DIM), jnp.float32), 'W1': init(ks[3], (DEPTH, DIM, 2 * DIM_INNER)), 'b1': jnp.zeros((DEPTH, 2 * DIM_INNER), jnp.float32), 'W2': init(ks[4], (DEPTH, DIM_INNER, DIM)), 'b2': jnp.zeros((DEPTH, DIM), jnp.float32)}
    _L0_ffn_in = _L0_ffn_setup()
    _d = {'L0_attn_x': _L0_attn_in['x'], 'L0_attn_w_kv_down': _L0_attn_in['w_kv_down'], 'L0_attn_w_kv_up': _L0_attn_in['w_kv_up'], 'L0_attn_w_q': _L0_attn_in['w_q'], 'L0_attn_w_out': _L0_attn_in['w_out'], 'L0_ffn_Wqkv': _L0_ffn_in['Wqkv'], 'L0_ffn_q_scale': _L0_ffn_in['q_scale'], 'L0_ffn_k_scale': _L0_ffn_in['k_scale'], 'L0_ffn_Wo': _L0_ffn_in['Wo'], 'L0_ffn_ln_g': _L0_ffn_in['ln_g'], 'L0_ffn_ln_b': _L0_ffn_in['ln_b'], 'L0_ffn_W1': _L0_ffn_in['W1'], 'L0_ffn_b1': _L0_ffn_in['b1'], 'L0_ffn_W2': _L0_ffn_in['W2'], 'L0_ffn_b2': _L0_ffn_in['b2']}
    _x0 = _d['L0_attn_x']
    _d['L0_attn_x'] = jax.random.normal(jax.random.fold_in(jax.random.key(seed), 1), (8, 256, 128), dtype=_x0.dtype)
    del _x0
    return _d

def reference(L0_attn_x, L0_attn_w_kv_down, L0_attn_w_kv_up, L0_attn_w_q, L0_attn_w_out, L0_ffn_Wqkv, L0_ffn_q_scale, L0_ffn_k_scale, L0_ffn_Wo, L0_ffn_ln_g, L0_ffn_ln_b, L0_ffn_W1, L0_ffn_b1, L0_ffn_W2, L0_ffn_b2):

    def _L0_attn_ref(x, w_kv_down, w_kv_up, w_q, w_out):
        import jax, jax.numpy as jnp
        import numpy as np
        B, T, C = (64, 32, 128)
        N_HEAD, HEAD_SIZE, KV_RANK = (16, 64, 128)
        BLOCK_SIZE = 32
        Bx, Tx, Cx = x.shape
        HD = N_HEAD * HEAD_SIZE
        latent_kv = x @ w_kv_down
        kv = latent_kv @ w_kv_up
        k, v = (kv[..., :HD], kv[..., HD:])
        k = k.reshape(Bx, Tx, N_HEAD, HEAD_SIZE)
        v = v.reshape(Bx, Tx, N_HEAD, HEAD_SIZE)
        q = (x @ w_q).reshape(Bx, Tx, N_HEAD, HEAD_SIZE)
        scale = HEAD_SIZE ** (-0.5)
        att = jnp.einsum('bqhd,bkhd->bhqk', q, k) * scale
        causal = jnp.tril(jnp.ones((Tx, Tx), dtype=bool))
        att = jnp.where(causal, att, -jnp.inf)
        att = jax.nn.softmax(att, axis=-1)
        y = jnp.einsum('bhqk,bkhd->bqhd', att, v)
        y = y.reshape(Bx, Tx, HD)
        return y @ w_out

    def _L0_ffn_ref(x, Wqkv, q_scale, k_scale, Wo, ln_g, ln_b, W1, b1, W2, b2):
        import jax, jax.numpy as jnp
        import numpy as np
        DIM = 128
        DEPTH = 6
        HEADS = 16
        DIM_HEAD = 64
        WINDOW = 32
        INNER = HEADS * DIM_HEAD
        DIM_INNER = int(DIM * 4 * 2 / 3)
        QK_SCALE = 8.0

        def shift_tokens(t):
            a, s = jnp.split(t, 2, -1)
            s = jnp.pad(s, ((0, 0), (1, 0), (0, 0)))[:, :-1]
            return jnp.concatenate([a, s], -1)

        def l2norm(t):
            return t / jnp.maximum(jnp.linalg.norm(t, axis=-1, keepdims=True), 1e-12)

        def rotate_half(x):
            x1, x2 = jnp.split(x, 2, -1)
            return jnp.concatenate([-x2, x1], -1)

        def rotary_tables(n):
            half = jnp.arange(0, DIM_HEAD, 2, dtype=jnp.float32)
            inv_freq = 1.0 / 10000.0 ** (half / DIM_HEAD)
            t = jnp.arange(n, dtype=jnp.float32)
            freqs = t[:, None] * inv_freq[None, :]
            freqs = jnp.concatenate([freqs, freqs], -1)
            base_scale = (half + 0.4 * DIM_HEAD) / (1.4 * DIM_HEAD)
            power = (t - n // 2) / (WINDOW // 2)
            scale = base_scale[None, :] ** power[:, None]
            scale = jnp.concatenate([scale, scale], -1)
            return (freqs, scale)

        def local_attention(q, k, v):
            b, h, n, d = q.shape
            w = WINDOW
            nw = n // w
            bq = q.reshape(b, h, nw, w, d)
            bk = k.reshape(b, h, nw, w, d)
            bv = v.reshape(b, h, nw, w, d)

            def look(t):
                p = jnp.pad(t, ((0, 0), (0, 0), (1, 0), (0, 0), (0, 0)))
                return jnp.concatenate([p[:, :, :nw], p[:, :, 1:]], axis=3)
            bk2, bv2 = (look(bk), look(bv))
            seq = jnp.arange(n).reshape(nw, w)
            seq_p = jnp.pad(seq, ((1, 0), (0, 0)), constant_values=-1)
            jt = jnp.concatenate([seq_p[:nw], seq_p[1:]], axis=1)
            it = seq[:, :, None]
            jb = jt[:, None, :]
            mask = (it < jb) | (it > jb + w) | (jb == -1)
            sim = jnp.einsum('bhwie,bhwje->bhwij', bq, bk2) * QK_SCALE
            sim = jnp.where(mask, -jnp.finfo(sim.dtype).max, sim)
            attn = jax.nn.softmax(sim, -1)
            out = jnp.einsum('bhwij,bhwje->bhwie', attn, bv2)
            return out.reshape(b, h, n, d)

        def attn_layer(x, Wqkv, qs, ksc, Wo):
            b, n, _ = x.shape
            qkv = x @ Wqkv
            q, k, v = jnp.split(qkv, 3, -1)
            sh = lambda t: t.reshape(b, n, HEADS, DIM_HEAD).transpose(0, 2, 1, 3)
            q, k, v = (sh(q), sh(k), sh(v))
            q = l2norm(q) * qs
            k = l2norm(k) * ksc
            freqs, scale = rotary_tables(n)
            cos, sin = (jnp.cos(freqs), jnp.sin(freqs))
            q = q * cos * scale + rotate_half(q) * sin * scale
            inv = 1.0 / scale
            k = k * cos * inv + rotate_half(k) * sin * inv
            out = local_attention(q, k, v)
            out = out.transpose(0, 2, 1, 3).reshape(b, n, INNER)
            return out @ Wo

        def ffn_layer(x, g, bln, W1, b1, W2, b2):
            mu = x.mean(-1, keepdims=True)
            var = ((x - mu) ** 2).mean(-1, keepdims=True)
            xn = (x - mu) / jnp.sqrt(var + 1e-05) * g + bln
            hg = xn @ W1 + b1
            a, gate = jnp.split(hg, 2, -1)
            return a * jax.nn.gelu(gate, approximate=False) @ W2 + b2
        for i in range(DEPTH):
            x = attn_layer(shift_tokens(x), Wqkv[i], q_scale[i], k_scale[i], Wo[i]) + x
            x = ffn_layer(shift_tokens(x), ln_g[i], ln_b[i], W1[i], b1[i], W2[i], b2[i]) + x
        return x
    x = L0_attn_x
    xn = _layernorm(x, axis=-1)
    x = x + _L0_attn_ref(xn, L0_attn_w_kv_down, L0_attn_w_kv_up, L0_attn_w_q, L0_attn_w_out) + _L0_ffn_ref(xn, L0_ffn_Wqkv, L0_ffn_q_scale, L0_ffn_k_scale, L0_ffn_Wo, L0_ffn_ln_g, L0_ffn_ln_b, L0_ffn_W1, L0_ffn_b1, L0_ffn_W2, L0_ffn_b2)
    return x

_drawn_inputs = setup_inputs


def setup_inputs(seed=0):
    import zlib

    import numpy as np

    out = dict(_drawn_inputs(seed))
    spreads = {'L0_ffn_q_scale': (1.0, 0.6),
     'L0_ffn_k_scale': (1.0, 0.6),
     'L0_ffn_ln_g': (1.0, 0.6),
     'L0_ffn_ln_b': (0.0, 0.8),
     'L0_ffn_b1': (0.0, 0.8),
     'L0_ffn_b2': (0.0, 0.1)}
    factors = {'L0_attn_w_kv_down': 3.757,
     'L0_attn_w_kv_up': 3.753,
     'L0_attn_w_q': 8.0,
     'L0_attn_w_out': 3.717,
     'L0_ffn_W1': 3.64,
     'L0_ffn_W2': 3.573}
    for name, (base, spread) in spreads.items():
        noise = np.random.default_rng([zlib.crc32(name.encode()), seed]).standard_normal(out[name].shape)
        drawn = base * np.exp(spread * noise) if base else spread * noise
        out[name] = jnp.asarray(drawn.astype(out[name].dtype))
    for name, factor in factors.items():
        out[name] = (out[name] * factor).astype(out[name].dtype)
    return out
```

```python
from contextlib import ExitStack

import numpy as np

import concourse.bass as bass
from concourse import mybir

F32 = mybir.dt.float32
BF16 = mybir.dt.bfloat16
ALU = mybir.AluOpType
ACT = mybir.ActivationFunctionType
AX_X = mybir.AxisListType.X
ds = bass.ds

P = 128
NB, T = 8, 256
TT = T // P
DEPTH = 6
H, D = 16, 64
G, HG = 4, 4
HD = H * D
GW = HG * D
STEPS = NB * G
WIN = 32
LN_EXP = "natural_log_exp_and_others"
INNER = P * 4 * 2 // 3
CW = [P, P, INNER - 2 * P]
PAIRS = NB // 2
N_SMALL = 4 * HG + 6 + 3
QK_SCALE = 8.0
NBIG = -1e30
LNS = 2.0 ** 30
ROOT = 2.0 ** 15
EPS = 1e-5
SPANS = {"causal": [(0, P), (0, 2 * P)], "local": [(0, P), (P - WIN, P + WIN)]}
PT_COLS = {"causal": 3 * P, "local": 2 * P + WIN}
PT_ON_DVE, PT_ON_ACT = (0, 2), (1, 3)
Q1, Q2, K1, K2, LG, LB, B2, BA, BG, NPAR = 0, 1, 2, 3, 4, 5, 6, 7, 10, 13

CONST = {}
_at = 0
for _name, _n in (("ident", P), ("mask_causal", 3 * P), ("mask_local", 2 * P + WIN), ("blk", P),
                  ("center", P), ("avg", P), ("rot", 4 * T)):
    CONST[_name] = (_at, _n)
    _at += _n
NCONST = _at


def constants():
    c = np.zeros((P, NCONST), np.float32)

    def put(name, a):
        at, n = CONST[name]
        c[:, at:at + n] = a

    i = np.arange(P)[:, None]
    put("ident", np.eye(P))
    masks = {}
    for kind in SPANS:
        parts = []
        for t, (k0, w) in enumerate(SPANS[kind]):
            q, k = i + P * t, k0 + np.arange(w)[None, :]
            ok = k <= q
            if kind == "local":
                ok = ok & (k >= q - WIN)
            parts.append(np.where(ok, 0.0, NBIG))
        masks[kind] = np.concatenate(parts, 1)
    put("mask_causal", masks["causal"])
    put("mask_local", masks["local"])
    put("blk", i // 32 == np.arange(P)[None, :] // 32)
    put("avg", np.full((P, P), 1.0 / P))
    put("center", np.eye(P) - 1.0 / P)
    half = np.arange(0, D, 2, dtype=np.float32)
    inv = (1.0 / np.float32(10000.0) ** (half / np.float32(D))).astype(np.float32)
    pos = np.arange(T, dtype=np.float32)
    freqs = (pos[None, :] * inv[:, None]).astype(np.float32).astype(np.float64)
    base = ((half + np.float32(0.4 * D)) / np.float32(1.4 * D)).astype(np.float64)
    scale = base[:, None] ** ((pos[None, :] - T // 2) / (WIN // 2)).astype(np.float64)
    cos, sin = np.cos(freqs), np.sin(freqs)
    rot = np.concatenate([cos * scale * (QK_SCALE * ROOT), sin * scale * (QK_SCALE * ROOT), cos / scale * ROOT, sin / scale * ROOT], 1)
    put("rot", np.tile(rot, (HG, 1)))
    return c


def build(nc, x, w_kv_down, w_kv_up, w_q, w_out, Wqkv, q_scale, k_scale, Wo, ln_g, ln_b, W1, b1, W2, b2, const, out):
    with ExitStack() as ctx:
        def sb(name, shape, dt=F32):
            return ctx.enter_context(nc.sbuf_tensor(name, shape, dt))

        def sem(name):
            return ctx.enter_context(nc.semaphore(name))

        consts = sb("consts", [P, NCONST])

        def con(name):
            at, n = CONST[name]
            return consts[:, at:at + n]

        ident = con("ident")
        ident_b = sb("ident_b", [P, P], BF16)
        mask_b = {"causal": sb("mask_causal_b", [P, 3 * P], BF16), "local": sb("mask_local_b", [P, 2 * P + WIN], BF16)}
        x_rows = sb("x_rows", [P, NB * TT, P])
        xn_rows = sb("xn_rows", [P, NB * TT, P])
        stats = sb("stats", [P, 4, NB * TT])
        xs = sb("xs", [P, NB, T + 1])
        attn = sb("attn", [P, NB, T])
        xh = sb("xh", [P, NB, T])
        xin = sb("xin", [P, T])
        latent = sb("latent", [P, T])
        wdown = sb("wdown", [P, P])
        wq = sb("wq", [P, HD])
        wk = sb("wk", [P, HD])
        wv = sb("wv", [P, HD])
        wo = sb("wo", [P, HD // P, P])
        w1 = sb("w1", [P, 2 * INNER])
        w2 = sb("w2", [P, 3, P])
        par_rows = sb("par_rows", [NPAR * DEPTH, P])
        pars = sb("pars", [P, NPAR, DEPTH])
        par = sb("par", [P, NPAR])
        tabs = sb("tabs", [P, 4, 2, T])
        rot_u = sb("rot_u", [P, 2, 2, T])
        rot_v = sb("rot_v", [P, 2, 2, T])
        sq = sb("sq", [P, 2, 2, T])
        sqs = sb("sqs", [P, 2, T])
        ln_n = sb("ln_n", [P, 2, T])
        rinv = sb("rinv", [P, 2, T])
        z_raw = sb("z_raw", [P, 2, 2, T])
        z_norm = sb("z_norm", [P, 2, 2, 2, T])
        zqk = sb("zqk", [P, G, 2, 2, T])
        v_sb = sb("v_sb", [P, TT, HD])
        nm = sb("nm", [P, HG, TT])
        probs = sb("probs", [P, HG, 3 * P])
        probs_t = sb("probs_t", [P, HG, 3 * P])
        rsum = sb("rsum", [P, HG, TT])
        rrec = sb("rrec", [P, HG, TT])
        yt = sb("yt", [P, HD // P, T])
        xc = sb("xc", [P, T])
        xc2 = sb("xc2", [P, T])
        ln_v = sb("ln_v", [P, T])
        rstd = sb("rstd", [P, T])
        gate = sb("gate", [P, 3, 2 * T])
        hid = sb("hid", [P, 3, 2 * T])
        tiny = sb("tiny", [P, 2])

        bank = [ctx.enter_context(nc.psum_tensor(f"bank{i}", [P, 512], F32)) for i in range(8)]
        B_S, B_Q, B_K, B_Y, B_N = bank[:4], bank[4], bank[5], bank[6], bank[7]

        names = """const_in x_in small_in wkv_down_in wqk_in wv_in wo_in w1_in w2_in out_dma
            tiny_ready zeros_ready masks_ready mean centred squared var_sum rstd_ln rstd_row xn_ready xnt_done xs_ready
            pars_turned pars_ready probs_zero par_ready tabs_ready xin_ready down_done latent_ready
            q_done k_done q_prod k_prod q_square k_square sums_ready zq_ready zk_ready k_summed q_summed zn_ready n_done ln_done rinv_ready
            z_in0 z_in1 z_in2 z_in3 v_done v_ready qk_done nm_ready exp_done rrec_ready pn_ready pt_tail_zero pt_done pt_dve pt_act pv_done
            yt_ready wo_done res_done xc_done xc_ready xc_squared var_done ln_var rstd_ready xh_raw xh_ready
            up_done gelu_done hid_ready mlp_done mlp_res fin_sum fin_done rows_ready""".split()
        S = {n: sem(n) for n in names}

        UP = [(bank[0], bank[1]), (bank[2], bank[3]), (B_K, B_N)]

        def after(eng, name, value):
            if not (isinstance(value, int) and value <= 0):
                eng.wait_ge(S[name], value)

        def credit(eng, per_step="", per_batch="", per_pair="", per_chunk=""):
            for name in per_step.split():
                eng.sem_inc(S[name], STEPS)
            for name in per_batch.split():
                eng.sem_inc(S[name], NB)
            for name in per_pair.split():
                eng.sem_inc(S[name], PAIRS)
            for name in per_chunk.split():
                eng.sem_inc(S[name], 3 * PAIRS)

        def z_landed(batches):
            return 16 * 2 * HG * batches

        def norms_due(g, has):
            return "s1" in has if g else "s2" in has

        def phase(eng, ph, body):
            body(ph, -1, ("s1",))
            body(ph, 0, ("s1", "s2"))
            with eng.Fori(1, NB - 1) as b:
                body(ph, b, ("s1", "s2", "post"))
            body(ph, NB - 1, ("s2", "post"))
            body(ph, NB, ("post",))

        block = ctx.enter_context(nc.Block())

        @block.sync
        def _(sp):
            sp.dma_start(consts[:, :], const).then_inc(S["const_in"], 16)
            sp.dma_start(x_rows[:, :, :], x.rearrange("b (t p) c -> p (b t) c", p=P)).then_inc(S["x_in"], 16)
            sp.dma_start(wdown[:, :], w_kv_down).then_inc(S["wkv_down_in"], 16)
            sp.dma_start(wq[:, :], w_q).then_inc(S["wqk_in"], 16)
            sp.dma_start(wk[:, :], w_kv_up[:, 0:HD]).then_inc(S["wqk_in"], 16)
            sp.dma_start(wv[:, :], w_kv_up[:, HD:2 * HD]).then_inc(S["wv_in"], 16)
            sp.dma_start(wo[:, :, :], w_out.rearrange("(c p) n -> p c n", p=P)).then_inc(S["wo_in"], 16)
            sp.dma_start(w1[:, :], W1[0, :, :]).then_inc(S["w1_in"], 16)
            sp.dma_start(w2[:, 0:2, :], W2[0, 0:2 * P, :].rearrange("(c p) n -> p c n", p=P)).then_inc(S["w2_in"], 16)
            sp.dma_start(w2[0:CW[2], 2, :], W2[0, 2 * P:INNER, :]).then_inc(S["w2_in"], 16)
            n_small = 0

            def small(dst, src):
                nonlocal n_small
                sp.dma_start(dst, src).then_inc(S["small_in"], 16)
                n_small += 1

            def param_rows(j):
                return par_rows[j * DEPTH:(j + 1) * DEPTH]

            sp.wait_ge(S["zeros_ready"], 2)
            for hh in range(HG):
                for half in range(2):
                    cols, own = slice(32 * hh, 32 * hh + 32), slice(32 * half, 32 * half + 32)
                    small(param_rows(Q1 + half)[:, cols], q_scale[:, own])
                    small(param_rows(K1 + half)[:, cols], k_scale[:, own])
            for c in range(3):
                for at, j in ((0, BA), (INNER, BG)):
                    small(param_rows(j + c)[:, 0:CW[c]], b1[:, at + c * P:at + c * P + CW[c]])
            for src, j in ((ln_g, LG), (ln_b, LB), (b2, B2)):
                small(param_rows(j), src)
            assert n_small == N_SMALL

            def attention_weights(l, phases):
                sp.wait_ge(S["v_done"], phases * STEPS)
                row = Wqkv[ds(l, 1), :, :].rearrange("a p n -> (a p) n")
                sp.dma_start(wq[:, :], row[:, 0:HD]).then_inc(S["wqk_in"], 16)
                sp.dma_start(wk[:, :], row[:, HD:2 * HD]).then_inc(S["wqk_in"], 16)
                sp.dma_start(wv[:, :], row[:, 2 * HD:3 * HD]).then_inc(S["wv_in"], 16)
                sp.wait_ge(S["wo_done"], phases * NB)
                sp.dma_start(wo[:, :, :], Wo[ds(l, 1), :, :].rearrange("a (c p) n -> p (a c) n", p=P)).then_inc(S["wo_in"], 16)

            def body(ph, b, has):
                i = ph * NB + b
                if "s1" not in has:
                    return
                for g in range(G):
                    n1 = (i + 1) * G + g
                    sp.wait_ge(S["zn_ready"], n1 + 1)
                    for h in range(HG):
                        for half in range(2):
                            to = 64 * (h % 2) + 32 * half
                            sp.dma_start(zqk[to:to + 32, g, :, h // 2, :], z_norm[32 * h:32 * h + 32, g % 2, :, half, :]).then_inc(S[f"z_in{g}"], 16)

            attention_weights(0, 1)
            phase(sp, 1, body)
            with sp.Fori(1, DEPTH) as l:
                attention_weights(l, l + 1)
                sp.wait_ge(S["mlp_done"], (l + 1) * PAIRS)
                sp.dma_start(w1[:, :], W1[ds(l, 1), :, :].rearrange("a p n -> (a p) n")).then_inc(S["w1_in"], 16)
                row = W2[ds(l, 1), :, :].rearrange("a p n -> (a p) n")
                sp.dma_start(w2[:, 0:2, :], row[0:2 * P, :].rearrange("(c p) n -> p c n", p=P)).then_inc(S["w2_in"], 16)
                sp.dma_start(w2[0:CW[2], 2, :], row[2 * P:INNER, :]).then_inc(S["w2_in"], 16)
                phase(sp, l + 1, body)
            for p in range(PAIRS):
                sp.wait_ge(S["rows_ready"], p + 1)
                b0 = 2 * p
                sp.dma_start(out[b0:b0 + 2, :, :].rearrange("b (t p) c -> p (b t) c", p=P),
                             xn_rows[:, TT * b0:TT * b0 + 2 * TT, :]).then_inc(S["out_dma"], 16)
            sp.wait_ge(S["out_dma"], 16 * PAIRS)

        @block.gpsimd
        def _(pool):
            pool.memset(tiny[:, 0:1], 2.0 ** -64).then_inc(S["tiny_ready"], 1)
            pool.wait_ge(S["tiny_ready"], 1)
            pool.memset(tiny[:, 1:2], EPS).then_inc(S["tiny_ready"], 1)
            pool.wait_ge(S["tiny_ready"], 2)
            pool.memset(xs[64:P, :, 0:1], 0.0).then_inc(S["zeros_ready"], 1)
            pool.wait_ge(S["zeros_ready"], 1)
            pool.memset(par_rows[:, :], 0.0).then_inc(S["zeros_ready"], 1)

            def body(ph, b, has):
                i = ph * NB + b
                if "s1" not in has:
                    return
                for g in range(G):
                    n1 = (i + 1) * G + g
                    pool.wait_ge(S["k_square"], n1 + 1)
                    pool.wait_ge(S["q_square"], n1 + 1)
                    pool.wait_ge(S["n_done"], n1)
                    pool.tensor_tensor(sqs[:, :, :], sq[:, :, 0, :], sq[:, :, 1, :], ALU.add).then_inc(S["sums_ready"], 1)
                    pool.wait_ge(S["zn_ready"], n1)
                    for idx, prod, mark in ((1, "k_prod", "k_summed"), (0, "q_prod", "q_summed")):
                        pool.wait_ge(S[prod], n1 + 1)
                        for half in range(2):
                            a = pool.tensor_tensor(z_raw[:, idx, half, :], rot_u[:, idx, half, :], rot_v[:, idx, 1 - half, :], ALU.add)
                        a.then_inc(S[mark], 1)

            pool.wait_ge(S["pt_done"], HG * STEPS)
            pool.memset(probs[:, :, P:2 * P - WIN], 0.0).then_inc(S["probs_zero"], 1)
            pool.wait_ge(S["pv_done"], STEPS)
            pool.memset(probs_t[:, :, P + P + WIN:3 * P], 0.0).then_inc(S["pt_tail_zero"], 1)
            credit(pool, per_step="k_summed q_summed sums_ready")
            with pool.Fori(0, DEPTH) as l:
                phase(pool, l + 1, body)

        @block.scalar
        def _(act):
            act.preload_act_table_set(LN_EXP)
            flat = xn_rows[:, :, :].rearrange("p a c -> p (a c)")
            act.wait_ge(S["centred"], 1)
            act.activation(xh[:, :, :].rearrange("p a c -> p (a c)"), flat, ACT.Square).then_inc(S["squared"], 1)
            act.wait_ge(S["tiny_ready"], 2)
            act.wait_ge(S["var_sum"], 1)
            act.activation(stats[:, 2, :], stats[:, 1, :], ACT.Ln, bias=tiny[:, 1:2], scale=1.0 / P).then_inc(S["rstd_ln"], 1)
            act.wait_ge(S["rstd_ln"], 1)
            act.activation(stats[:, 3, :], stats[:, 2, :], ACT.Exp, scale=-0.5).then_inc(S["rstd_row"], 1)

            def exps(kind, n, g):
                for h in range(HG):
                    act.wait_ge(S["nm_ready"], HG * n + h + 1)
                    at = 0
                    for t, (k0, w) in enumerate(SPANS[kind]):
                        a = act.activation(probs[:, h, t * P + k0:t * P + k0 + w], B_S[h][:, at:at + w], ACT.Exp,
                                           bias=nm[:, h, t:t + 1],
                                           accum_out=rsum[:, h, t:t + 1])
                        at += w
                    a.then_inc(S["exp_done"], 1)

            def yt_out(i, g):
                n = i * G + g
                act.wait_ge(S["pv_done"], n + 1)
                after(act, "wo_done", i)
                act.activation(yt[:, 2 * g:2 * g + 2, :], B_Y[:, :].rearrange("p (c t) -> p c t", c=2), ACT.Copy).then_inc(S["yt_ready"], 1)

            def v_out(n1, g):
                act.wait_ge(S["v_done"], n1 + 1)
                after(act, "pv_done", n1 + 1 - G)
                act.activation(v_sb[:, :, g * GW:(g + 1) * GW], B_N[:, :].rearrange("p (t n) -> p t n", t=TT), ACT.Copy).then_inc(S["v_ready"], 1)

            def squares(n1, which):
                done, bankx, idx, mark = (("k_done", B_K, 1, "k_square"), ("q_done", B_Q, 0, "q_square"))[which]
                act.wait_ge(S[done], n1 + 1)
                act.wait_ge(S["sums_ready"], n1)
                act.activation(sq[:, idx, :, :], bankx[:, :].rearrange("p (a t) -> p a t", a=2), ACT.Square).then_inc(S[mark], 1)

            def body(kind, ph, b, has):
                i = ph * NB + b
                s1, s2, post = ("s1" in has), ("s2" in has), ("post" in has)
                for g in range(G):
                    n, n1 = i * G + g, (i + 1) * G + g
                    if s2 and g:
                        yt_out(i, g - 1)
                    if post and g == 0:
                        yt_out(i - 1, G - 1)
                    if norms_due(g, has):
                        v_out(n1 - 1, (g - 1) % G)
                    if s2:
                        exps(kind, n, g)
                    if post and kind == "local" and g == 2:
                        act.wait_ge(S["xc_ready"], i)
                        after(act, "var_done", i - 1)
                        act.activation(xc2[:, :], xc[:, :], ACT.Square).then_inc(S["xc_squared"], 1)
                    if post and kind == "local" and g == 3:
                        act.wait_ge(S["var_done"], i)
                        act.activation(ln_v[:, :], B_Q[:, 0:T], ACT.Ln, bias=tiny[:, 1:2]).then_inc(S["ln_var"], 1)
                        act.wait_ge(S["ln_var"], i)
                        after(act, "xh_raw", i - 1)
                        act.activation(rstd[:, :], ln_v[:, :], ACT.Exp, scale=-0.5).then_inc(S["rstd_ready"], 1)
                    if s1 and kind == "causal":
                        if g == 0:
                            act.wait_ge(S["down_done"], i + 2)
                            after(act, "v_done", n1)
                            act.activation(latent[:, :], B_N[:, 0:T], ACT.Copy).then_inc(S["latent_ready"], 1)
                        act.wait_ge(S["q_done"], n1 + 1)
                        after(act, "qk_done", HG * (n1 + 1 - G))
                        act.activation(zqk[:, g, 0, :, :], B_Q[:, :].rearrange("p (a t) -> p a t", a=2), ACT.Copy, scale=D ** -0.5).then_inc(S["zq_ready"], 1)
                    if s1 and kind == "local":
                        squares(n1, 0)
                    if kind == "local" and norms_due(g, has):
                        act.wait_ge(S["n_done"], n1)
                        act.activation(ln_n[:, :, :], B_N[:, :].rearrange("p (a t) -> p a t", a=2), ACT.Ln, bias=tiny[:, 0:1], scale=LNS).then_inc(S["ln_done"], 1)
                        act.wait_ge(S["ln_done"], n1)
                        act.wait_ge(S["zn_ready"], n1 - 1)
                        act.activation(rinv[:, :, :], ln_n[:, :, :], ACT.Exp, scale=-0.5).then_inc(S["rinv_ready"], 1)
                    if s1 and kind == "local":
                        squares(n1, 1)
                    if s2:
                        for h in PT_ON_ACT:
                            act.wait_ge(S["pt_done"], HG * n + h + 1)
                            after(act, "pv_done", n)
                            act.activation(probs_t[:, h, 0:PT_COLS[kind]], B_S[h][:, 0:PT_COLS[kind]], ACT.Copy).then_inc(S["pt_act"], 1)

            phase(act, 0, lambda ph, b, has: body("causal", ph, b, has))

            def gelus(m):
                for c in range(3):
                    act.wait_ge(S["up_done"], 3 * m + c + 1)
                    after(act, "hid_ready", 3 * (m - 1) + c + 1)
                    act.activation(gate[0:CW[c], c, :], UP[c][1][0:CW[c], :], ACT.Gelu, bias=par[0:CW[c], BG + c:BG + c + 1]).then_inc(S["gelu_done"], 1)

            credit(act, per_step="q_square k_square ln_done rinv_ready", per_batch="xc_squared ln_var rstd_ready", per_chunk="gelu_done")
            with act.Fori(0, DEPTH) as l:
                act.preload_act_table_set(LN_EXP)
                phase(act, l + 1, lambda ph, b, has: body("local", ph, b, has))
                act.preload_act_table(ACT.Gelu)
                with act.Fori(0, PAIRS) as p:
                    gelus((l + 1) * PAIRS + p)

        @block.tensor
        def _(pe):
            pe.wait_ge(S["const_in"], 16)
            pe.wait_ge(S["masks_ready"], 3)
            pe.wait_ge(S["xn_ready"], 1)
            for p in range(PAIRS):
                for k in range(2 * TT):
                    m = pe.transpose(bank[p][:, k * P:(k + 1) * P], xn_rows[:, 2 * TT * p + k, :], ident)
                m.then_inc(S["xnt_done"], 1)
            pe.wait_ge(S["small_in"], 16 * N_SMALL)
            pe.transpose(B_Q[:, 0:NPAR * DEPTH], par_rows[:, :], ident[0:NPAR * DEPTH, 0:NPAR * DEPTH]).then_inc(S["pars_turned"], 1)
            pe.wait_ge(S["pars_ready"], 1)
            pe.wait_ge(S["wkv_down_in"], 16)

            def pt_taken(n, h):
                name, heads = ("pt_dve", PT_ON_DVE) if h in PT_ON_DVE else ("pt_act", PT_ON_ACT)
                after(pe, name, len(heads) * n + heads.index(h) + 1)

            def qk(kind, i, g):
                n = i * G + g
                if kind == "causal":
                    pe.wait_ge(S["zq_ready"], n + 1)
                    pe.wait_ge(S["zk_ready"], n + 1)
                else:
                    pe.wait_ge(S[f"z_in{g}"], z_landed(i - NB + 1))
                spans = SPANS[kind]
                w_all = sum(w for _, w in spans)
                for pair in range(2):
                    heads = (2 * pair, 2 * pair + 1)
                    for h in heads:
                        pt_taken(n - 1, h)
                        pe.matmul(B_S[h][:, 0:w_all], ident_b[:, :], mask_b[kind][:, :], start=True, stop=True)
                    at = 0
                    for t, (k0, w) in enumerate(spans):
                        for h in heads:
                            r = slice(D * (h % 2), D * (h % 2) + D)
                            m = pe.matmul(B_S[h][:, at:at + w], zqk[r, g, 0, pair, t * P:(t + 1) * P], zqk[r, g, 1, pair, k0:k0 + w],
                                          start=False, stop=True, tile_position=(D * (h % 2), 0), skip_group_check=True)
                            if t == TT - 1:
                                m.then_inc(S["qk_done"], 1)
                        at += w

            def norms(n1):
                pe.wait_ge(S["v_ready"], n1 + 1)
                pe.wait_ge(S["sums_ready"], n1 + 1)
                pe.matmul(B_N[:, :], con("blk"), sqs[:, :, :].rearrange("p a t -> p (a t)"), start=True, stop=True).then_inc(S["n_done"], 1)

            def values(kind, n1, g):
                if kind == "causal":
                    after(pe, "v_ready", n1)
                else:
                    pe.wait_ge(S["ln_done"], n1)
                src = latent if kind == "causal" else xin
                for t in range(TT):
                    m = pe.matmul(B_N[:, t * GW:(t + 1) * GW], src[:, t * P:(t + 1) * P], wv[:, g * GW:(g + 1) * GW], start=True, stop=True)
                m.then_inc(S["v_done"], 1)

            def q_taken(kind, n):
                if kind == "causal":
                    after(pe, "zq_ready", n)
                else:
                    pe.wait_ge(S["q_prod"], n)
                    pe.wait_ge(S["q_square"], n)

            def k_taken(kind, n):
                if kind == "causal":
                    after(pe, "zk_ready", n)
                else:
                    pe.wait_ge(S["k_prod"], n)
                    pe.wait_ge(S["k_square"], n)

            def project(bankx, w, g, src, mark):
                for half in range(2):
                    at = g * GW + half * P
                    m = pe.matmul(bankx[:, half * T:(half + 1) * T], w[:, at:at + P], src[:, :], start=True, stop=True)
                m.then_inc(S[mark], 1)

            def output_projection(ph, i):
                pe.wait_ge(S["wo_in"], 16 * (ph + 1))
                pe.wait_ge(S["yt_ready"], G * i)
                for c in range(HD // P):
                    m = pe.matmul(B_Q[:, 0:T], wo[:, c, :], yt[:, c, :], start=(c == 0), stop=(c == HD // P - 1))
                m.then_inc(S["wo_done"], 1)

            def body(kind, ph, b, has):
                i = ph * NB + b
                s1, s2, post = ("s1" in has), ("s2" in has), ("post" in has)
                for g in range(G):
                    n, n1 = i * G + g, (i + 1) * G + g
                    if s2:
                        qk(kind, i, g)
                    if post and g:
                        q_taken(kind, n1 if s1 else i * G + G if s2 else i * G)
                    if post and g == 1:
                        output_projection(ph, i)
                        if kind == "local" and not s2:
                            up(ph, 0)
                    if post and kind == "local" and g == 2:
                        pe.wait_ge(S["res_done"], i)
                        pe.matmul(B_Q[:, 0:T], con("center"), xs[:, ds(b - 1, 1), 0:T].rearrange("p a t -> p (a t)"), start=True, stop=True).then_inc(S["xc_done"], 1)
                    if post and kind == "local" and g == 3:
                        pe.wait_ge(S["xc_squared"], i)
                        pe.matmul(B_Q[:, 0:T], con("avg"), xc2[:, :], start=True, stop=True).then_inc(S["var_done"], 1)
                    if s1:
                        if g == 0:
                            pe.wait_ge(S["xin_ready"], i + 2)
                            pe.wait_ge(S["wqk_in"], 32 * (ph + 1))
                            pe.wait_ge(S["wv_in"], 16 * (ph + 1))
                            if kind == "causal":
                                after(pe, "v_ready", n1)
                                pe.matmul(B_N[:, 0:T], wdown[:, :], xin[:, :], start=True, stop=True).then_inc(S["down_done"], 1)
                                pe.wait_ge(S["latent_ready"], i + 2)
                        k_taken(kind, n1)
                        project(B_K, wk, g, latent if kind == "causal" else xin, "k_done")
                    if kind == "local" and norms_due(g, has):
                        norms(n1 - 1)
                    if s1:
                        q_taken(kind, n1)
                        if post and g == 1:
                            pe.wait_ge(S["res_done"], i)
                        if post and kind == "local" and g == 2:
                            pe.wait_ge(S["xc_ready"], i)
                        if post and kind == "local" and g == 3:
                            pe.wait_ge(S["ln_var"], i)
                        project(B_Q, wq, g, xin, "q_done")
                    if s2:
                        for h in range(HG):
                            pe.wait_ge(S["pn_ready"], HG * n + h + 1)
                            late = P if kind == "causal" else WIN
                            pe.transpose(B_S[h][:, 0:P], probs[:, h, 2 * P:3 * P], ident)
                            pe.transpose(B_S[h][:, P:2 * P], probs[:, h, 0:P], ident)
                            pe.transpose(B_S[h][:, 2 * P:2 * P + late], probs[0:late, h, P:2 * P], ident[0:late, 0:late]).then_inc(S["pt_done"], 1)
                        after(pe, "yt_ready", n)
                        pe.wait_ge(S["v_ready"], n + 1)
                        for h in range(HG):
                            pt_taken(n, h)
                            f = slice(g * GW + h * D, g * GW + (h + 1) * D)
                            rows, at = slice(D * (h % 2), D * (h % 2) + D), T * (h // 2)
                            pe.matmul(B_Y[rows, at:at + T], v_sb[:, 0, f], probs_t[:, h, P:3 * P], start=True, stop=True,
                                      tile_position=(0, D * (h % 2)), skip_group_check=True)
                            m = pe.matmul(B_Y[rows, at + P:at + T], v_sb[:, 1, f], probs_t[:, h, 0:P], start=False, stop=True,
                                          tile_position=(0, D * (h % 2)), skip_group_check=True)
                        m.then_inc(S["pv_done"], 1)
                    if s1:
                        values(kind, n1, g)

            def up(ph, p):
                m = ph * PAIRS + p
                pe.wait_ge(S["w1_in"], 16 * ph)
                pe.wait_ge(S["xh_ready"], ph * NB + 2 * p + 2)
                first = isinstance(p, int)
                if first:
                    n = (ph + 1) * STEPS
                    pe.wait_ge(S["pt_dve"], len(PT_ON_DVE) * n)
                    pe.wait_ge(S["pt_act"], len(PT_ON_ACT) * n)
                    k_taken("local", n)
                    pe.wait_ge(S["v_ready"], n)
                rhs = xh[:, ds(2 * p, 2), :].rearrange("p a t -> p (a t)")
                for c in range(3):
                    if not first:
                        pe.wait_ge(S["hid_ready"], 3 * (m - 1) + c + 1)
                    for k, at in ((0, 0), (1, INNER)):
                        mm = pe.matmul(UP[c][k][0:CW[c], :], w1[:, at + c * P:at + c * P + CW[c]], rhs, start=True, stop=True)
                    mm.then_inc(S["up_done"], 1)

            def down(ph, p):
                m = ph * PAIRS + p
                pe.wait_ge(S["w2_in"], 32 * ph)
                if isinstance(p, int):
                    pe.wait_ge(S["yt_ready"], (ph + 1) * STEPS)
                else:
                    pe.wait_ge(S["mlp_res"], m)
                pe.wait_ge(S["hid_ready"], 3 * m + 3)
                for c in range(3):
                    mm = pe.matmul(B_Y[:, :], w2[0:CW[c], c, :], hid[0:CW[c], c, :], start=(c == 0), stop=(c == 2))
                mm.then_inc(S["mlp_done"], 1)

            phase(pe, 0, lambda ph, b, has: body("causal", ph, b, has))
            pe.wait_ge(S["probs_zero"], 1)
            pe.wait_ge(S["pt_tail_zero"], 1)
            pe.wait_ge(S["zq_ready"], STEPS)
            pe.wait_ge(S["zk_ready"], STEPS)
            credit(pe, per_step="n_done", per_batch="xc_done var_done", per_pair="mlp_done", per_chunk="up_done")
            with pe.Fori(0, DEPTH) as l:
                pe.wait_ge(S["hid_ready"], 3 * PAIRS * (l + 1))
                pe.wait_ge(S["mlp_res"], PAIRS * (l + 1))
                phase(pe, l + 1, lambda ph, b, has: body("local", ph, b, has))
                down(l + 1, 0)
                with pe.Fori(1, PAIRS) as p:
                    up(l + 1, p)
                    down(l + 1, p)
            for p in range(PAIRS):
                pe.wait_ge(S["fin_sum"], p + 1)
                for k in range(2 * TT):
                    m = pe.transpose(bank[p][:, k * P:(k + 1) * P], xh[:, 2 * p + k // 2, (k % 2) * P:(k % 2 + 1) * P], ident)
                m.then_inc(S["fin_done"], 1)

        @block.vector
        def _(dve):
            dve.wait_ge(S["const_in"], 16)
            dve.tensor_copy(ident_b[:, :], ident).then_inc(S["masks_ready"], 1)
            dve.tensor_copy(mask_b["causal"][:, :], con("mask_causal")).then_inc(S["masks_ready"], 1)
            dve.tensor_copy(mask_b["local"][:, :], con("mask_local")).then_inc(S["masks_ready"], 1)
            NT = NB * TT
            dve.wait_ge(S["x_in"], 16)
            dve.tensor_reduce(stats[:, 0, :], x_rows[:, :, :], AX_X, ALU.add).then_inc(S["mean"], 1)
            dve.wait_ge(S["mean"], 1)
            dve.tensor_scalar(stats[:, 1, :], stats[:, 0, :], 1.0 / P, None, ALU.mult).then_inc(S["mean"], 1)
            dve.wait_ge(S["mean"], 2)
            dve.tensor_tensor(xn_rows[:, :, :], x_rows[:, :, :], stats[:, 1, :].unsqueeze(2).broadcast_to([P, NT, P]), ALU.subtract).then_inc(S["centred"], 1)
            dve.wait_ge(S["squared"], 1)
            dve.tensor_reduce(stats[:, 1, :], xh[:, :, :].rearrange("p a (t c) -> p (a t) c", c=P), AX_X, ALU.add).then_inc(S["var_sum"], 1)
            dve.wait_ge(S["rstd_row"], 1)
            dve.tensor_tensor(xn_rows[:, :, :], xn_rows[:, :, :], stats[:, 3, :].unsqueeze(2).broadcast_to([P, NT, P]), ALU.mult).then_inc(S["xn_ready"], 1)
            dve.wait_ge(S["zeros_ready"], 2)
            for p in range(PAIRS):
                dve.wait_ge(S["xnt_done"], p + 1)
                src = bank[p][:, :].rearrange("p (a t) -> p a t", a=2)
                dve.tensor_copy(xs[0:64, 2 * p:2 * p + 2, 0:T], src[0:64]).then_inc(S["xs_ready"], 1)
                dve.tensor_copy(xs[64:P, 2 * p:2 * p + 2, 1:T + 1], src[64:P]).then_inc(S["xs_ready"], 1)

            dve.wait_ge(S["pars_turned"], 1)
            dve.tensor_copy(pars[:, :, :], B_Q[:, 0:NPAR * DEPTH].rearrange("p (j l) -> p j l", j=NPAR)).then_inc(S["pars_ready"], 1)

            def maxima(kind, n):
                for h in range(HG):
                    dve.wait_ge(S["qk_done"], HG * n + h + 1)
                    at = 0
                    for t, (k0, w) in enumerate(SPANS[kind]):
                        m = dve.tensor_reduce(nm[:, h, t:t + 1], B_S[h][:, at:at + w], AX_X, ALU.max, negate=True)
                        at += w
                    m.then_inc(S["nm_ready"], 1)

            def probabilities(kind, n, pair):
                heads = slice(2 * pair, 2 * pair + 2)
                dve.wait_ge(S["exp_done"], HG * n + 2 * pair + 2)
                dve.reciprocal(rrec[:, heads, :], rsum[:, heads, :]).then_inc(S["rrec_ready"], 1)
                dve.wait_ge(S["rrec_ready"], 2 * n + pair + 1)
                for h in (2 * pair, 2 * pair + 1):
                    for t, (k0, w) in enumerate(SPANS[kind]):
                        seen = probs[:, h, t * P + k0:t * P + k0 + w]
                        m = dve.tensor_scalar(seen, seen, rrec[:, h, t:t + 1], None, ALU.mult)
                    m.then_inc(S["pn_ready"], 1)

            def rotate(n1, idx):
                squared, bankx, mark, taken = (("q_square", B_Q, "q_prod", "q_summed"), ("k_square", B_K, "k_prod", "k_summed"))[idx]
                dve.wait_ge(S[squared], n1 + 1)
                dve.wait_ge(S[taken], n1)
                src = bankx[:, :].rearrange("p (a t) -> p a t", a=2)
                dve.tensor_tensor(rot_u[:, idx, :, :], src, tabs[:, 2 * idx, :, :], ALU.mult)
                dve.tensor_tensor(rot_v[:, idx, :, :], src, tabs[:, 2 * idx + 1, :, :], ALU.mult).then_inc(S[mark], 1)

            def normalise(j, g):
                n1 = j * G + g
                dve.wait_ge(S["rinv_ready"], n1 + 1)
                dve.wait_ge(S[f"z_in{(g - 2) % G}"], z_landed(j - NB + (1 if g >= 2 else 0)))
                for idx, summed in ((1, "k_summed"), (0, "q_summed")):
                    dve.wait_ge(S[summed], n1 + 1)
                    m = dve.scalar_tensor_tensor(out=z_norm[:, g % 2, idx, :, :], in0=rinv[:, idx, :].unsqueeze(1).broadcast_to([P, 2, T]),
                                                 scalar=1e12 / ROOT, in1=z_raw[:, idx, :, :], op0=ALU.min, op1=ALU.mult)
                m.then_inc(S["zn_ready"], 1)

            def body(kind, ph, b, has):
                i = ph * NB + b
                s1, s2, post = ("s1" in has), ("s2" in has), ("post" in has)
                if s1:
                    after(dve, "v_done", (i + 1) * G)
                    src = xs[:, ds(b + 1, 1), :].rearrange("p a t -> p (a t)")
                    if kind == "causal":
                        dve.tensor_copy(xin[0:64, :], src[0:64, 0:T])
                        dve.tensor_copy(xin[64:P, :], src[64:P, 1:T + 1]).then_inc(S["xin_ready"], 1)
                    else:
                        dve.tensor_copy(xin[:, :], src[:, 0:T]).then_inc(S["xin_ready"], 1)
                for g in range(G):
                    n, n1 = i * G + g, (i + 1) * G + g
                    if s2:
                        maxima(kind, n)
                    if post and g == 1:
                        dve.wait_ge(S["wo_done"], i)
                        if kind == "causal":
                            dve.tensor_copy(attn[:, ds(b - 1, 1), :].rearrange("p a t -> p (a t)"), B_Q[:, 0:T]).then_inc(S["res_done"], 1)
                        else:
                            lo = xs[0:64, ds(b - 1, 1), 0:T].rearrange("p a t -> p (a t)")
                            hi = xs[64:P, ds(b - 1, 1), 1:T + 1].rearrange("p a t -> p (a t)")
                            dve.tensor_tensor(lo, B_Q[0:64, 0:T], lo, ALU.add)
                            dve.tensor_tensor(hi, B_Q[64:P, 0:T], hi, ALU.add).then_inc(S["res_done"], 1)
                    if post and kind == "local" and g == 2:
                        dve.wait_ge(S["xc_done"], i)
                        dve.tensor_copy(xc[:, :], B_Q[:, 0:T]).then_inc(S["xc_ready"], 1)
                    if s1 and kind == "causal":
                        dve.wait_ge(S["k_done"], n1 + 1)
                        after(dve, "qk_done", HG * (n1 + 1 - G))
                        dve.tensor_copy(zqk[:, g, 1, :, :], B_K[:, :].rearrange("p (a t) -> p a t", a=2)).then_inc(S["zk_ready"], 1)
                    if s2:
                        probabilities(kind, n, 0)
                        probabilities(kind, n, 1)
                        for h in PT_ON_DVE:
                            dve.wait_ge(S["pt_done"], HG * n + h + 1)
                            after(dve, "pv_done", n)
                            dve.tensor_copy(probs_t[:, h, 0:PT_COLS[kind]], B_S[h][:, 0:PT_COLS[kind]]).then_inc(S["pt_dve"], 1)
                    if s1 and kind == "local":
                        rotate(n1, 1)
                        rotate(n1, 0)
                    if kind == "local" and norms_due(g, has):
                        normalise(i + 1 if g else i, (g - 1) % G)
                    if post and kind == "local" and g == 3:
                        dve.wait_ge(S["rstd_ready"], i)
                        dve.tensor_tensor(xc[:, :], xc[:, :], rstd[:, :], ALU.mult).then_inc(S["xh_raw"], 1)
                        dve.wait_ge(S["xh_raw"], i)
                        dve.tensor_scalar(xh[:, ds(b - 1, 1), :].rearrange("p a t -> p (a t)"), xc[:, :], par[:, LG:LG + 1], par[:, LB:LB + 1],
                                          ALU.mult, ALU.add).then_inc(S["xh_ready"], 1)

            dve.wait_ge(S["xs_ready"], 2 * PAIRS)
            phase(dve, 0, lambda ph, b, has: body("causal", ph, b, has))

            def hidden(m):
                for c in range(3):
                    dve.wait_ge(S["gelu_done"], 3 * m + c + 1)
                    after(dve, "mlp_done", m)
                    dve.scalar_tensor_tensor(out=hid[0:CW[c], c, :], in0=UP[c][0][0:CW[c], :], scalar=par[0:CW[c], BA + c:BA + c + 1],
                                             in1=gate[0:CW[c], c, :], op0=ALU.add, op1=ALU.mult).then_inc(S["hid_ready"], 1)

            def residual(m, p):
                dve.wait_ge(S["mlp_done"], m + 1)
                src = B_Y[:, :].rearrange("p (a t) -> p a t", a=2)
                for rows, at in ((slice(0, 64), 0), (slice(64, P), 1)):
                    dst = xs[rows, ds(2 * p, 2), at:at + T]
                    a = dve.scalar_tensor_tensor(out=dst, in0=src[rows], scalar=par[rows, B2:B2 + 1], in1=dst, op0=ALU.add, op1=ALU.add)
                a.then_inc(S["mlp_res"], 1)

            credit(dve, per_step="q_prod k_prod zn_ready", per_batch="xc_ready xh_raw xh_ready", per_pair="mlp_res", per_chunk="hid_ready")
            with dve.Fori(0, DEPTH) as l:
                dve.wait_ge(S["mlp_res"], (l + 1) * PAIRS)
                dve.tensor_copy(par[:, :], pars[:, :, ds(l, 1)].rearrange("p n a -> p (n a)")).then_inc(S["par_ready"], 1)
                dve.wait_ge(S["par_ready"], l + 1)
                for k, (c1, sign) in enumerate(((Q1, 1), (Q1, -1), (K1, 1), (K1, -1))):
                    for half in range(2):
                        m = dve.tensor_scalar(tabs[:, k, half, :], con("rot")[:, k * T:(k + 1) * T], par[:, c1 + half:c1 + half + 1],
                                              float(sign if half else 1), ALU.mult, ALU.mult)
                m.then_inc(S["tabs_ready"], 1)
                dve.wait_ge(S["tabs_ready"], l + 1)
                phase(dve, l + 1, lambda ph, b, has: body("local", ph, b, has))
                with dve.Fori(0, PAIRS) as p:
                    m = (l + 1) * PAIRS + p
                    hidden(m)
                    residual(m, p)
            dve.wait_ge(S["mlp_res"], (DEPTH + 1) * PAIRS)
            for p in range(PAIRS):
                for rows, at in ((slice(0, 64), 0), (slice(64, P), 1)):
                    a = dve.tensor_tensor(xh[rows, 2 * p:2 * p + 2, :], xs[rows, 2 * p:2 * p + 2, at:at + T], attn[rows, 2 * p:2 * p + 2, :], ALU.add)
                a.then_inc(S["fin_sum"], 1)
            for p in range(PAIRS):
                dve.wait_ge(S["fin_done"], p + 1)
                tiles = slice(2 * TT * p, 2 * TT * (p + 1))
                dve.tensor_tensor(xn_rows[:, tiles, :], bank[p][:, :].rearrange("p (k c) -> p k c", c=P), x_rows[:, tiles, :], ALU.add).then_inc(S["rows_ready"], 1)


_INS = ["L0_attn_x", "L0_attn_w_kv_down", "L0_attn_w_kv_up", "L0_attn_w_q", "L0_attn_w_out", "L0_ffn_Wqkv",
        "L0_ffn_q_scale", "L0_ffn_k_scale", "L0_ffn_Wo", "L0_ffn_ln_g", "L0_ffn_ln_b", "L0_ffn_W1", "L0_ffn_b1",
        "L0_ffn_W2", "L0_ffn_b2"]


def kernel(**inputs):
    import concourse.bacc as bacc
    from concourse.bass_utils import run_bass_kernel_spmd

    nc = bacc.Bacc("TRN2", target_bir_lowering=False, num_devices=1)
    arrays = {f"in_{name}": np.ascontiguousarray(inputs[name]) for name in _INS}
    arrays["in_constants"] = constants()
    for name, ranges in (("L0_ffn_Wqkv", 2),):
        a = arrays[f"in_{name}"].copy()
        for k in range(ranges):
            part = a[..., k * HD:(k + 1) * HD].reshape(*a.shape[:-1], G, HG, 2, D // 2)
            a[..., k * HD:(k + 1) * HD] = np.moveaxis(part, -2, -3).reshape(*a.shape[:-1], HD)
        arrays[f"in_{name}"] = a
    args = [nc.dram_tensor(n, a.shape, F32, kind="ExternalInput").ap() for n, a in arrays.items()]
    out = nc.dram_tensor("out_0", (NB, T, P), F32, kind="ExternalOutput").ap()
    build(nc, *args, out)
    r = run_bass_kernel_spmd(nc, [arrays], core_ids=[0])
    return r.results[0]["out_0"]
```

```python
from contextlib import ExitStack

import numpy as np

import concourse.bass as bass
from concourse import mybir

F32 = mybir.dt.float32
BF16 = mybir.dt.bfloat16
ALU = mybir.AluOpType
ACT = mybir.ActivationFunctionType
AX_X = mybir.AxisListType.X
ds = bass.ds

P = 128
NB, T = 8, 256
TT = T // P
DEPTH = 6
H, D = 16, 64
G, HG = 4, 4
HD = H * D
GW = HG * D
STEPS = NB * G
WIN = 32
LN_EXP = "natural_log_exp_and_others"
INNER = P * 4 * 2 // 3
CW = [P, P, INNER - 2 * P]
PAIRS = NB // 2
N_SMALL = 4 * HG + 6 + 3
QK_SCALE = 8.0
NBIG = -1e30
LNS = 2.0 ** 30
ROOT = 2.0 ** 15
EPS = 1e-5
SPANS = {"causal": [(0, P), (0, 2 * P)], "local": [(0, P), (P - WIN, P + WIN)]}
PT_COLS = {"causal": 3 * P, "local": 2 * P + WIN}
PT_ON_DVE, PT_ON_ACT = (0, 2), (1, 3)
Q1, Q2, K1, K2, LG, LB, B2, BA, BG, NPAR = 0, 1, 2, 3, 4, 5, 6, 7, 10, 13

CONST = {}
_at = 0
for _name, _n in (("ident", P), ("mask_causal", 3 * P), ("mask_local", 2 * P + WIN), ("blk", P),
                  ("center", P), ("avg", P), ("rot", 4 * T)):
    CONST[_name] = (_at, _n)
    _at += _n
NCONST = _at


def constants():
    c = np.zeros((P, NCONST), np.float32)

    def put(name, a):
        at, n = CONST[name]
        c[:, at:at + n] = a

    i = np.arange(P)[:, None]
    put("ident", np.eye(P))
    masks = {}
    for kind in SPANS:
        parts = []
        for t, (k0, w) in enumerate(SPANS[kind]):
            q, k = i + P * t, k0 + np.arange(w)[None, :]
            ok = k <= q
            if kind == "local":
                ok = ok & (k >= q - WIN)
            parts.append(np.where(ok, 0.0, NBIG))
        masks[kind] = np.concatenate(parts, 1)
    put("mask_causal", masks["causal"])
    put("mask_local", masks["local"])
    put("blk", i // 32 == np.arange(P)[None, :] // 32)
    put("avg", np.full((P, P), 1.0 / P))
    put("center", np.eye(P) - 1.0 / P)
    half = np.arange(0, D, 2, dtype=np.float32)
    inv = (1.0 / np.float32(10000.0) ** (half / np.float32(D))).astype(np.float32)
    pos = np.arange(T, dtype=np.float32)
    freqs = (pos[None, :] * inv[:, None]).astype(np.float32).astype(np.float64)
    base = ((half + np.float32(0.4 * D)) / np.float32(1.4 * D)).astype(np.float64)
    scale = base[:, None] ** ((pos[None, :] - T // 2) / (WIN // 2)).astype(np.float64)
    cos, sin = np.cos(freqs), np.sin(freqs)
    rot = np.concatenate([cos * scale * (QK_SCALE * ROOT), sin * scale * (QK_SCALE * ROOT), cos / scale * ROOT, sin / scale * ROOT], 1)
    put("rot", np.tile(rot, (HG, 1)))
    return c


def build(nc, x, w_kv_down, w_kv_up, w_q, w_out, Wqkv, q_scale, k_scale, Wo, ln_g, ln_b, W1, b1, W2, b2, const, out):
    with ExitStack() as ctx:
        def sb(name, shape, dt=F32):
            return ctx.enter_context(nc.sbuf_tensor(name, shape, dt))

        def sem(name):
            return ctx.enter_context(nc.semaphore(name))

        consts = sb("consts", [P, NCONST])

        def con(name):
            at, n = CONST[name]
            return consts[:, at:at + n]

        ident = con("ident")
        ident_b = sb("ident_b", [P, P], BF16)
        mask_b = {"causal": sb("mask_causal_b", [P, 3 * P], BF16), "local": sb("mask_local_b", [P, 2 * P + WIN], BF16)}
        x_rows = sb("x_rows", [P, NB * TT, P])
        xn_rows = sb("xn_rows", [P, NB * TT, P])
        stats = sb("stats", [P, 4, NB * TT])
        xs = sb("xs", [P, NB, T + 1])
        attn = sb("attn", [P, NB, T])
        xh = sb("xh", [P, NB, T])
        xin = sb("xin", [P, T])
        latent = sb("latent", [P, T])
        wdown = sb("wdown", [P, P])
        wq = sb("wq", [P, HD])
        wk = sb("wk", [P, HD])
        wv = sb("wv", [P, HD])
        wo = sb("wo", [P, HD // P, P])
        w1 = sb("w1", [P, 2 * INNER])
        w2 = sb("w2", [P, 3, P])
        par_rows = sb("par_rows", [NPAR * DEPTH, P])
        pars = sb("pars", [P, NPAR, DEPTH])
        par_rot = sb("par_rot", [P, LG])
        par = sb("par", [P, NPAR - LG])
        tabs = sb("tabs", [P, 4, 2, T])
        rot_u = sb("rot_u", [P, 2, 2, T])
        rot_v = sb("rot_v", [P, 2, 2, T])
        sq = sb("sq", [P, 2, 2, T])
        sqs = sb("sqs", [P, 2, T])
        ln_n = sb("ln_n", [P, 2, T])
        rinv = sb("rinv", [P, 2, T])
        z_raw = sb("z_raw", [P, 2, 2, T])
        z_norm = sb("z_norm", [P, 2, 2, 2, T])
        zqk = sb("zqk", [P, G, 2, 2, T])
        v_sb = sb("v_sb", [P, 2, TT, HD])
        nm = sb("nm", [P, HG, TT])
        probs = sb("probs", [P, HG, 3 * P])
        probs_t = sb("probs_t", [P, HG, 3 * P])
        rsum = sb("rsum", [P, HG, TT])
        rrec = sb("rrec", [P, HG, TT])
        yt = sb("yt", [P, HD // P, T])
        xc = sb("xc", [P, T])
        xc2 = sb("xc2", [P, T])
        ln_v = sb("ln_v", [P, T])
        rstd = sb("rstd", [P, T])
        gate = sb("gate", [P, 3, T])
        hid = sb("hid", [P, 3, T])
        tiny = sb("tiny", [P, 2])

        bank = [ctx.enter_context(nc.psum_tensor(f"bank{i}", [P, 512], F32)) for i in range(8)]
        B_S, B_Q, B_K, B_Y, B_N = bank[:4], bank[4], bank[5], bank[6], bank[7]

        names = """const_in x_in small_in wkv_down_in wqk_in wv_in wo_in w1_in w2_in out_dma
            tiny_ready zeros_ready masks_ready mean centred squared var_sum rstd_ln rstd_row xn_ready xnt_done xt_ready xs_ready
            pars_turned pars_ready probs_zero par_rot_ready par_ready tabs_ready xin_ready down_done latent_ready
            q_done k_done q_prod k_prod q_square k_square sums_ready zq_ready zk_ready k_summed q_summed inv_norm_ready zn_ready n_done ln_done rinv_ready
            z_in0 z_in1 z_in2 z_in3 v_done v_ready qk_done nm_ready exp_done rrec_ready pn_ready pt_done pt_dve pt_act pv_done
            yt_ready wo_done res_done xc_done xc_ready xc_squared var_done ln_var rstd_ready xh_raw xh_ready
            up_done gelu_done hid_ready mlp_done mlp_res fin_sum fin_done rows_ready""".split()
        S = {n: sem(n) for n in names}

        MLP_LATE = ((B_K, B_N, B_K), B_Q)
        MLP_TURN = ((bank[0], bank[1], bank[2]), B_Y)
        EARLY, AMID = (0, 2, 4, 5), (1, 3, None, None)

        def after(eng, name, value):
            if not (isinstance(value, int) and value <= 0):
                eng.wait_ge(S[name], value)

        def credit(eng, per_step="", per_batch="", per_chunk=""):
            for name in per_step.split():
                eng.sem_inc(S[name], STEPS)
            for name in per_batch.split():
                eng.sem_inc(S[name], NB)
            for name in per_chunk.split():
                eng.sem_inc(S[name], 3 * NB)

        def z_landed(batches):
            return 16 * 2 * HG * batches

        def stage1_batch(i, has):
            return i if "turn" in has else i + 1

        def stage1_odd(odd, has):
            return odd if "turn" in has else 1 - odd

        def norms_due(g, has):
            return "s1" in has if g else "s2" in has

        def late_pair(g, has):
            return "s2" in has if g else "post" in has

        def first_batch(step, ph):
            for g in range(G):
                step(ph, -1, ("s1",), g, 1)

        def middle(eng, step, ph):
            for g in range(G):
                step(ph, 0, ("s1", "s2"), g, 0)
            with eng.Fori(0, NB // 2 - 1) as r:
                for odd in (1, 0):
                    for g in range(G):
                        step(ph, 2 * r + 2 - odd, ("s1", "s2", "post"), g, odd)

        def last_batch(step, ph, has=("s2", "post")):
            for g in range(G):
                step(ph, NB - 1, has, g, 1)

        def turn(step, ph, has):
            for g in range(G):
                step(ph, NB, has, g, 0)

        def layers(eng, step, start=None, between=None):
            def layer(l, has):
                if start:
                    start(l)
                middle(eng, step, l + 1)
                last_batch(step, l + 1, ("s2", "post", "mlp"))
                if between and "s1" in has:
                    between(l)
                turn(step, l + 1, has)

            with eng.Fori(0, DEPTH - 1) as l:
                layer(l, ("s1", "post", "mlp", "turn"))
            layer(DEPTH - 1, ("post", "mlp", "turn"))

        block = ctx.enter_context(nc.Block())

        @block.sync
        def _(sp):
            sp.dma_start(consts[:, :], const).then_inc(S["const_in"], 16)
            sp.dma_start(x_rows[:, :, :], x.rearrange("b (t p) c -> p (b t) c", p=P)).then_inc(S["x_in"], 16)
            sp.dma_start(wdown[:, :], w_kv_down).then_inc(S["wkv_down_in"], 16)
            sp.dma_start(wq[:, :], w_q).then_inc(S["wqk_in"], 16)
            sp.dma_start(wk[:, :], w_kv_up[:, 0:HD]).then_inc(S["wqk_in"], 16)
            sp.dma_start(wv[:, :], w_kv_up[:, HD:2 * HD]).then_inc(S["wv_in"], 16)
            sp.dma_start(wo[:, :, :], w_out.rearrange("(c p) n -> p c n", p=P)).then_inc(S["wo_in"], 16)
            sp.dma_start(w1[:, :], W1[0, :, :]).then_inc(S["w1_in"], 16)
            sp.dma_start(w2[:, 0:2, :], W2[0, 0:2 * P, :].rearrange("(c p) n -> p c n", p=P)).then_inc(S["w2_in"], 16)
            sp.dma_start(w2[0:CW[2], 2, :], W2[0, 2 * P:INNER, :]).then_inc(S["w2_in"], 16)
            n_small = 0

            def small(dst, src):
                nonlocal n_small
                sp.dma_start(dst, src).then_inc(S["small_in"], 16)
                n_small += 1

            def param_rows(j):
                return par_rows[j * DEPTH:(j + 1) * DEPTH]

            sp.wait_ge(S["zeros_ready"], 2)
            for hh in range(HG):
                for half in range(2):
                    cols, own = slice(32 * hh, 32 * hh + 32), slice(32 * half, 32 * half + 32)
                    small(param_rows(Q1 + half)[:, cols], q_scale[:, own])
                    small(param_rows(K1 + half)[:, cols], k_scale[:, own])
            for c in range(3):
                for at, j in ((0, BA), (INNER, BG)):
                    small(param_rows(j + c)[:, 0:CW[c]], b1[:, at + c * P:at + c * P + CW[c]])
            for src, j in ((ln_g, LG), (ln_b, LB), (b2, B2)):
                small(param_rows(j), src)
            assert n_small == N_SMALL

            def qkv_weights(l):
                sp.wait_ge(S["v_done"], (l + 1) * STEPS)
                row = Wqkv[ds(l, 1), :, :].rearrange("a p n -> (a p) n")
                sp.dma_start(wq[:, :], row[:, 0:HD]).then_inc(S["wqk_in"], 16)
                sp.dma_start(wk[:, :], row[:, HD:2 * HD]).then_inc(S["wqk_in"], 16)
                sp.dma_start(wv[:, :], row[:, 2 * HD:3 * HD]).then_inc(S["wv_in"], 16)

            def out_weights(l):
                sp.wait_ge(S["wo_done"], (l + 1) * NB)
                sp.dma_start(wo[:, :, :], Wo[ds(l, 1), :, :].rearrange("a (c p) n -> p (a c) n", p=P)).then_inc(S["wo_in"], 16)

            def mlp_weights(l):
                sp.wait_ge(S["mlp_done"], (l + 1) * NB)
                sp.dma_start(w1[:, :], W1[ds(l, 1), :, :].rearrange("a p n -> (a p) n")).then_inc(S["w1_in"], 16)
                row = W2[ds(l, 1), :, :].rearrange("a p n -> (a p) n")
                sp.dma_start(w2[:, 0:2, :], row[0:2 * P, :].rearrange("(c p) n -> p c n", p=P)).then_inc(S["w2_in"], 16)
                sp.dma_start(w2[0:CW[2], 2, :], row[2 * P:INNER, :]).then_inc(S["w2_in"], 16)

            def step(ph, b, has, g, odd):
                i = ph * NB + b
                if "s1" not in has:
                    return
                n1 = stage1_batch(i, has) * G + g
                if "turn" in has and g == 1:
                    out_weights(ph)
                if "turn" in has and g == G - 1:
                    mlp_weights(ph)
                sp.wait_ge(S["zn_ready"], n1 + 1)
                for h in range(HG):
                    for half in range(2):
                        to = 64 * (h % 2) + 32 * half
                        sp.dma_start(zqk[to:to + 32, g, :, h // 2, :], z_norm[32 * h:32 * h + 32, g % 2, :, half, :]).then_inc(S[f"z_in{g}"], 16)

            qkv_weights(0)
            out_weights(0)
            first_batch(step, 1)
            layers(sp, step, between=lambda l: qkv_weights(l + 1))
            for p in range(PAIRS):
                sp.wait_ge(S["rows_ready"], p + 1)
                b0 = 2 * p
                sp.dma_start(out[b0:b0 + 2, :, :].rearrange("b (t p) c -> p (b t) c", p=P),
                             xn_rows[:, TT * b0:TT * b0 + 2 * TT, :]).then_inc(S["out_dma"], 16)
            sp.wait_ge(S["out_dma"], 16 * PAIRS)

        @block.gpsimd
        def _(pool):
            pool.memset(tiny[:, 0:1], 2.0 ** -64).then_inc(S["tiny_ready"], 1)
            pool.wait_ge(S["tiny_ready"], 1)
            pool.memset(tiny[:, 1:2], EPS).then_inc(S["tiny_ready"], 1)
            pool.wait_ge(S["tiny_ready"], 2)
            pool.memset(xs[64:P, :, 0:1], 0.0).then_inc(S["zeros_ready"], 1)
            pool.wait_ge(S["zeros_ready"], 1)
            pool.memset(par_rows[:, :], 0.0).then_inc(S["zeros_ready"], 1)

            def normalise(j, g, idx):
                n1 = j * G + g
                if idx == 1:
                    pool.wait_ge(S["inv_norm_ready"], n1 + 1)
                    after(pool, f"z_in{(g - 2) % G}", z_landed(j - NB + (1 if g >= 2 else 0)))
                pool.wait_ge(S[("q_summed", "k_summed")[idx]], n1 + 1)
                m = pool.tensor_tensor(z_norm[:, g % 2, idx, :, :], rinv[:, idx, :].unsqueeze(1).broadcast_to([P, 2, T]), z_raw[:, idx, :, :], ALU.mult)
                if idx == 0:
                    m.then_inc(S["zn_ready"], 1)

            def step(ph, b, has, g, odd):
                i = ph * NB + b
                batch = stage1_batch(i, has)
                n1 = batch * G + g
                if norms_due(g, has):
                    normalise(batch if g else batch - 1, (g - 1) % G, 1)
                if "s1" in has:
                    pool.wait_ge(S["k_square"], n1 + 1)
                    pool.wait_ge(S["q_square"], n1 + 1)
                    pool.wait_ge(S["n_done"], n1)
                    pool.tensor_tensor(sqs[:, :, :], sq[:, :, 0, :], sq[:, :, 1, :], ALU.add).then_inc(S["sums_ready"], 1)
                if norms_due(g, has):
                    normalise(batch if g else batch - 1, (g - 1) % G, 0)
                if "s1" in has:
                    pool.wait_ge(S["zn_ready"], n1)
                    for idx, prod, mark in ((1, "k_prod", "k_summed"), (0, "q_prod", "q_summed")):
                        pool.wait_ge(S[prod], n1 + 1)
                        for half in range(2):
                            a = pool.tensor_tensor(z_raw[:, idx, half, :], rot_u[:, idx, half, :], rot_v[:, idx, 1 - half, :], ALU.add)
                        a.then_inc(S[mark], 1)

            pool.wait_ge(S["pt_done"], HG * STEPS)
            pool.memset(probs[:, :, P:2 * P - WIN], 0.0).then_inc(S["probs_zero"], 1)
            credit(pool, per_step="k_summed q_summed sums_ready zn_ready")
            first_batch(step, 1)
            layers(pool, step)

        @block.scalar
        def _(act):
            act.preload_act_table_set(LN_EXP)
            flat = xn_rows[:, :, :].rearrange("p a c -> p (a c)")
            act.wait_ge(S["centred"], 1)
            act.activation(xh[:, :, :].rearrange("p a c -> p (a c)"), flat, ACT.Square).then_inc(S["squared"], 1)
            act.wait_ge(S["tiny_ready"], 2)
            act.wait_ge(S["var_sum"], 1)
            act.activation(stats[:, 2, :], stats[:, 1, :], ACT.Ln, bias=tiny[:, 1:2], scale=1.0 / P).then_inc(S["rstd_ln"], 1)
            act.wait_ge(S["rstd_ln"], 1)
            act.activation(stats[:, 3, :], stats[:, 2, :], ACT.Exp, scale=-0.5).then_inc(S["rstd_row"], 1)

            for p in range(PAIRS):
                act.wait_ge(S["down_done"], p + 1)
                act.wait_ge(S["var_sum"], 1)
                act.activation(xh[:, 2 * p:2 * p + 2, :], bank[p][:, :].rearrange("p (a t) -> p a t", a=2), ACT.Copy).then_inc(S["latent_ready"], 1)

            def exps(kind, n, pair):
                for h in (2 * pair, 2 * pair + 1):
                    act.wait_ge(S["nm_ready"], HG * n + h + 1)
                    at = 0
                    for t, (k0, w) in enumerate(SPANS[kind]):
                        a = act.activation(probs[:, h, t * P + k0:t * P + k0 + w], B_S[h][:, at:at + w], ACT.Exp,
                                           bias=nm[:, h, t:t + 1], accum_out=rsum[:, h, t:t + 1])
                        at += w
                    a.then_inc(S["exp_done"], 1)

            def pt_out(kind, n, pair):
                for h in PT_ON_ACT:
                    if h // 2 == pair:
                        act.wait_ge(S["pt_done"], HG * n + h + 1)
                        after(act, "pv_done", n)
                        act.activation(probs_t[:, h, 0:PT_COLS[kind]], B_S[h][:, 0:PT_COLS[kind]], ACT.Copy).then_inc(S["pt_act"], 1)

            def yt_out(i, g):
                n = i * G + g
                act.wait_ge(S["pv_done"], n + 1)
                after(act, "wo_done", i)
                act.activation(yt[:, 2 * g:2 * g + 2, :], B_Y[:, :].rearrange("p (c t) -> p c t", c=2), ACT.Copy).then_inc(S["yt_ready"], 1)

            def v_out(n1, g, odd):
                act.wait_ge(S["v_done"], n1 + 1)
                after(act, "pv_done", n1 + 1 - 2 * G)
                act.activation(v_sb[:, odd, :, g * GW:(g + 1) * GW], B_N[:, :].rearrange("p (t n) -> p t n", t=TT), ACT.Copy).then_inc(S["v_ready"], 1)

            def squares(n1, which):
                done, bankx, idx, mark = (("k_done", B_K, 1, "k_square"), ("q_done", B_Q, 0, "q_square"))[which]
                act.wait_ge(S[done], n1 + 1)
                act.wait_ge(S["sums_ready"], n1)
                act.activation(sq[:, idx, :, :], bankx[:, :].rearrange("p (a t) -> p a t", a=2), ACT.Square).then_inc(S[mark], 1)

            def gelus(m, banks):
                for c in range(3):
                    act.wait_ge(S["up_done"], 3 * m + c + 1)
                    act.wait_ge(S["hid_ready"], 3 * (m - 1) + c + 1)
                    act.activation(gate[0:CW[c], c, :], banks[c][0:CW[c], T:2 * T], ACT.Gelu, bias=par[0:CW[c], BG - LG + c:BG - LG + c + 1]).then_inc(S["gelu_done"], 1)

            def step(kind, ph, b, has, g, odd):
                i = ph * NB + b
                s1, s2, post = ("s1" in has), ("s2" in has), ("post" in has)
                n, n1 = i * G + g, stage1_batch(i, has) * G + g
                mlp, m, late = "mlp" in has, ph * NB, late_pair(g, has)
                if norms_due(g, has):
                    v_out(n1 - 1, (g - 1) % G, stage1_odd(odd, has) if g else 1 - stage1_odd(odd, has))
                if late:
                    pt_out(kind, n - 1, 1)
                if s2:
                    exps(kind, n, 0)
                if s1 and kind == "local":
                    squares(n1, 0)
                if kind == "local" and norms_due(g, has):
                    act.wait_ge(S["n_done"], n1)
                    act.activation(ln_n[:, :, :], B_N[:, :].rearrange("p (a t) -> p a t", a=2), ACT.Ln, bias=tiny[:, 0:1], scale=LNS).then_inc(S["ln_done"], 1)
                    act.wait_ge(S["ln_done"], n1)
                    act.wait_ge(S["zn_ready"], n1 - 1)
                    act.activation(rinv[:, :, :], ln_n[:, :, :], ACT.Exp, scale=-0.5).then_inc(S["rinv_ready"], 1)
                if post and kind == "local" and g == 2:
                    act.wait_ge(S["xc_ready"], i)
                    after(act, "var_done", i - 1)
                    act.activation(xc2[:, :], xc[:, :], ACT.Square).then_inc(S["xc_squared"], 1)
                if post and kind == "local" and g == 3:
                    act.wait_ge(S["var_done"], i)
                    act.activation(ln_v[:, :], B_Q[:, 0:T], ACT.Ln, bias=tiny[:, 1:2]).then_inc(S["ln_var"], 1)
                    act.wait_ge(S["ln_var"], i)
                    after(act, "xh_raw", i - 1)
                    act.activation(rstd[:, :], ln_v[:, :], ACT.Exp, scale=-0.5).then_inc(S["rstd_ready"], 1)
                if late:
                    yt_out(i if g else i - 1, (g - 1) % G)
                if mlp and not s2 and g == 0:
                    act.preload_act_table(ACT.Gelu)
                    gelus(m + NB - 2, MLP_TURN[0])
                    act.preload_act_table_set(LN_EXP)
                if s2:
                    pt_out(kind, n, 0)
                    exps(kind, n, 1)
                if s1 and kind == "causal":
                    act.wait_ge(S["q_done"], n1 + 1)
                    after(act, "qk_done", HG * (n1 + 1 - G))
                    act.activation(zqk[:, g, 0, :, :], B_Q[:, :].rearrange("p (a t) -> p a t", a=2), ACT.Copy, scale=D ** -0.5).then_inc(S["zq_ready"], 1)
                if s1 and kind == "local":
                    squares(n1, 1)
                if mlp and s2:
                    act.preload_act_table(ACT.Gelu)
                    gelus(m + EARLY[g], MLP_LATE[0])
                if mlp and s2:
                    if AMID[g] is not None:
                        gelus(m + AMID[g], MLP_LATE[0])
                    act.preload_act_table_set(LN_EXP)
                if mlp and not s2 and g == G - 1:
                    act.preload_act_table(ACT.Gelu)
                    gelus(m + NB - 1, MLP_TURN[0])
                    act.preload_act_table_set(LN_EXP)

            causal = lambda ph, b, has, g, odd: step("causal", ph, b, has, g, odd)
            local = lambda ph, b, has, g, odd: step("local", ph, b, has, g, odd)
            first_batch(causal, 0)
            middle(act, causal, 0)
            last_batch(causal, 0)
            turn(causal, 0, ("post",))
            credit(act, per_step="q_square k_square ln_done rinv_ready", per_batch="xc_squared ln_var rstd_ready", per_chunk="gelu_done")
            act.preload_act_table_set(LN_EXP)
            first_batch(local, 1)
            layers(act, local)

        @block.tensor
        def _(pe):
            pe.wait_ge(S["const_in"], 16)
            pe.wait_ge(S["masks_ready"], 3)
            pe.wait_ge(S["xn_ready"], 1)
            for p in range(PAIRS):
                for k in range(2 * TT):
                    m = pe.transpose(bank[p][:, k * P:(k + 1) * P], xn_rows[:, 2 * TT * p + k, :], ident)
                m.then_inc(S["xnt_done"], 1)
            pe.wait_ge(S["wkv_down_in"], 16)
            for p in range(PAIRS):
                pe.wait_ge(S["xt_ready"], p + 1)
                pe.wait_ge(S["xs_ready"], 2 * p + 2)
                pe.matmul(bank[p][:, :], wdown[:, :], attn[:, 2 * p:2 * p + 2, :].rearrange("p a t -> p (a t)"), start=True, stop=True).then_inc(S["down_done"], 1)
            pe.wait_ge(S["small_in"], 16 * N_SMALL)
            pe.transpose(B_Q[:, 0:NPAR * DEPTH], par_rows[:, :], ident[0:NPAR * DEPTH, 0:NPAR * DEPTH]).then_inc(S["pars_turned"], 1)
            pe.wait_ge(S["pars_ready"], 1)
            pe.wait_ge(S["latent_ready"], PAIRS)

            def pt_taken(n, h):
                name, heads = ("pt_dve", PT_ON_DVE) if h in PT_ON_DVE else ("pt_act", PT_ON_ACT)
                after(pe, name, len(heads) * n + heads.index(h) + 1)

            def scores(kind, i, g, pair):
                n = i * G + g
                if pair == 0:
                    if kind == "causal":
                        pe.wait_ge(S["zq_ready"], n + 1)
                        pe.wait_ge(S["zk_ready"], n + 1)
                    else:
                        pe.wait_ge(S[f"z_in{g}"], z_landed(i - NB + 1))
                spans = SPANS[kind]
                w_all = sum(w for _, w in spans)
                heads = (2 * pair, 2 * pair + 1)
                for h in heads:
                    pt_taken(n - 1, h)
                    pe.matmul(B_S[h][:, 0:w_all], ident_b[:, :], mask_b[kind][:, :], start=True, stop=True)
                at = 0
                for t, (k0, w) in enumerate(spans):
                    for h in heads:
                        r = slice(D * (h % 2), D * (h % 2) + D)
                        mm = pe.matmul(B_S[h][:, at:at + w], zqk[r, g, 0, pair, t * P:(t + 1) * P], zqk[r, g, 1, pair, k0:k0 + w],
                                       start=False, stop=True, tile_position=(D * (h % 2), 0), skip_group_check=True)
                        if t == TT - 1:
                            mm.then_inc(S["qk_done"], 1)
                    at += w

            def transpose_probs(kind, n, pair):
                late = P if kind == "causal" else WIN
                for h in (2 * pair, 2 * pair + 1):
                    pe.wait_ge(S["pn_ready"], HG * n + h + 1)
                    pe.transpose(B_S[h][:, 0:P], probs[:, h, 2 * P:3 * P], ident)
                    pe.transpose(B_S[h][:, P:2 * P], probs[:, h, 0:P], ident)
                    pe.transpose(B_S[h][:, 2 * P:2 * P + late], probs[0:late, h, P:2 * P], ident[0:late, 0:late]).then_inc(S["pt_done"], 1)

            def weigh_values(kind, n, g, pair, odd):
                late = P if kind == "causal" else WIN
                if pair == 0:
                    after(pe, "yt_ready", n)
                    pe.wait_ge(S["v_ready"], n + 1)
                for h in (2 * pair, 2 * pair + 1):
                    pt_taken(n, h)
                    f = slice(g * GW + h * D, g * GW + (h + 1) * D)
                    rows, at = slice(D * (h % 2), D * (h % 2) + D), T * pair
                    pe.matmul(B_Y[rows, at:at + P + late], v_sb[:, odd, 0, f], probs_t[:, h, P:2 * P + late], start=True, stop=True,
                              tile_position=(0, D * (h % 2)), skip_group_check=True)
                    mm = pe.matmul(B_Y[rows, at + P:at + T], v_sb[:, odd, 1, f], probs_t[:, h, 0:P], start=False, stop=True,
                                   tile_position=(0, D * (h % 2)), skip_group_check=True)
                if pair == 1:
                    mm.then_inc(S["pv_done"], 1)

            def norms(n1):
                pe.wait_ge(S["v_ready"], n1 + 1)
                pe.wait_ge(S["sums_ready"], n1 + 1)
                pe.matmul(B_N[:, :], con("blk"), sqs[:, :, :].rearrange("p a t -> p (a t)"), start=True, stop=True).then_inc(S["n_done"], 1)

            def values(kind, n1, g):
                if kind == "causal":
                    after(pe, "v_ready", n1)
                else:
                    pe.wait_ge(S["ln_done"], n1)
                src = latent if kind == "causal" else xin
                for t in range(TT):
                    m = pe.matmul(B_N[:, t * GW:(t + 1) * GW], src[:, t * P:(t + 1) * P], wv[:, g * GW:(g + 1) * GW], start=True, stop=True)
                m.then_inc(S["v_done"], 1)

            def q_taken(kind, n):
                if kind == "causal":
                    after(pe, "zq_ready", n)
                else:
                    pe.wait_ge(S["q_prod"], n)
                    pe.wait_ge(S["q_square"], n)

            def k_taken(kind, n):
                if kind == "causal":
                    after(pe, "zk_ready", n)
                else:
                    pe.wait_ge(S["k_prod"], n)
                    pe.wait_ge(S["k_square"], n)

            def project(bankx, w, g, src, mark):
                for half in range(2):
                    at = g * GW + half * P
                    m = pe.matmul(bankx[:, half * T:(half + 1) * T], w[:, at:at + P], src, start=True, stop=True)
                m.then_inc(S[mark], 1)

            def output_projection(ph, i):
                pe.wait_ge(S["wo_in"], 16 * (ph + 1))
                pe.wait_ge(S["yt_ready"], G * i)
                for c in range(HD // P):
                    m = pe.matmul(B_Q[:, 0:T], wo[:, c, :], yt[:, c, :], start=(c == 0), stop=(c == HD // P - 1))
                m.then_inc(S["wo_done"], 1)

            def up(m, b, ph, banks):
                pe.wait_ge(S["w1_in"], 16 * ph)
                pe.wait_ge(S["xh_ready"], m + 1)
                for c in range(3):
                    pe.wait_ge(S["hid_ready"], 3 * m if banks[c] is not banks[0] or c == 0 else 3 * m + c - 1)
                    for k, at in ((0, 0), (1, INNER)):
                        mm = pe.matmul(banks[c][0:CW[c], k * T:(k + 1) * T], w1[:, at + c * P:at + c * P + CW[c]], xh[:, b, :], start=True, stop=True)
                    mm.then_inc(S["up_done"], 1)

            def down(m, ph, out_bank):
                pe.wait_ge(S["w2_in"], 32 * ph)
                pe.wait_ge(S["mlp_res"], m)
                pe.wait_ge(S["hid_ready"], 3 * m + 3)
                for c in range(3):
                    mm = pe.matmul(out_bank[:, 0:T], w2[0:CW[c], c, :], hid[0:CW[c], c, :], start=(c == 0), stop=(c == 2))
                mm.then_inc(S["mlp_done"], 1)

            def post_taken(kind, i, g):
                if g == 1:
                    pe.wait_ge(S["res_done"], i)
                if kind == "local" and g == 2:
                    pe.wait_ge(S["xc_ready"], i)
                if kind == "local" and g == 3:
                    pe.wait_ge(S["ln_var"], i)

            def step(kind, ph, b, has, g, odd):
                i = ph * NB + b
                s1, s2, post = ("s1" in has), ("s2" in has), ("post" in has)
                n, n1 = i * G + g, stage1_batch(i, has) * G + g
                mlp, m, late = "mlp" in has, ph * NB, late_pair(g, has)
                s1_ph, n1_batch = ph + 1 if "turn" in has else ph, stage1_batch(i, has)
                if s2:
                    scores(kind, i, g, 0)
                if late:
                    transpose_probs(kind, n - 1, 1)
                if kind == "local" and norms_due(g, has):
                    norms(n1 - 1)
                if mlp and s2:
                    if g == 0:
                        q_taken("local", n1)
                    else:
                        post_taken(kind, i, g - 1)
                    if g and AMID[g - 1] is not None:
                        down(m + AMID[g - 1], ph, MLP_LATE[1])
                    if g:
                        pe.wait_ge(S["mlp_res"], m + EARLY[g])
                if post and g:
                    q_taken(kind, n1 if s1 else i * G + G if s2 else i * G)
                if post and g == 1:
                    output_projection(ph, i)
                if post and kind == "local" and g == 2:
                    pe.wait_ge(S["res_done"], i)
                    pe.matmul(B_Q[:, 0:T], con("center"), xs[:, ds(b - 1, 1), 0:T].rearrange("p a t -> p (a t)"), start=True, stop=True).then_inc(S["xc_done"], 1)
                if post and kind == "local" and g == 3:
                    pe.wait_ge(S["xc_squared"], i)
                    pe.matmul(B_Q[:, 0:T], con("avg"), xc2[:, :], start=True, stop=True).then_inc(S["var_done"], 1)
                if s1:
                    if g == 0:
                        if kind == "local":
                            pe.wait_ge(S["xin_ready"], n1_batch + 1)
                        pe.wait_ge(S["wqk_in"], 32 * (s1_ph + 1))
                        pe.wait_ge(S["wv_in"], 16 * (s1_ph + 1))
                        if "turn" in has:
                            pe.wait_ge(S["hid_ready"], 3 * (m + NB - 2))
                            pe.wait_ge(S["mlp_res"], m + NB - 2)
                    k_taken(kind, n1)
                    project(B_K, wk, g, xh[:, ds(b + 1, 1), :].rearrange("p a t -> p (a t)") if kind == "causal" else xin[:, :], "k_done")
                if late:
                    weigh_values(kind, n - 1, (g - 1) % G, 1, odd if g else 1 - odd)
                if mlp and not s2 and g == 0:
                    for h in range(HG):
                        pt_taken(n - 1, h)
                    up(m + NB - 2, NB - 2, ph, MLP_TURN[0])
                if s2:
                    scores(kind, i, g, 1)
                    transpose_probs(kind, n, 0)
                if s1:
                    q_taken(kind, n1)
                    if post:
                        post_taken(kind, i, g)
                    project(B_Q, wq, g, attn[:, ds(b + 1, 1), :].rearrange("p a t -> p (a t)") if kind == "causal" else xin[:, :], "q_done")
                if mlp and s2:
                    if g == 0:
                        k_taken("local", n1)
                        pe.wait_ge(S["ln_done"], n1)
                    up(m + EARLY[g], EARLY[g], ph, MLP_LATE[0])
                if mlp and s2:
                    post_taken(kind, i, g)
                    down(m + EARLY[g], ph, MLP_LATE[1])
                if s2:
                    weigh_values(kind, n, g, 0, odd)
                if mlp and s2 and AMID[g] is not None:
                    up(m + AMID[g], AMID[g], ph, MLP_LATE[0])
                if s1:
                    if kind == "causal" and g == 0:
                        pe.wait_ge(S["xin_ready"], n1_batch + 1)
                    values(kind, n1, g)
                if mlp and not s2 and g == 0:
                    pe.wait_ge(S["yt_ready"], i * G)
                    down(m + NB - 2, ph, MLP_TURN[1])
                if mlp and not s2 and g == G - 1:
                    up(m + NB - 1, NB - 1, ph, MLP_TURN[0])
                    down(m + NB - 1, ph, MLP_TURN[1])

            causal = lambda ph, b, has, g, odd: step("causal", ph, b, has, g, odd)
            local = lambda ph, b, has, g, odd: step("local", ph, b, has, g, odd)
            first_batch(causal, 0)
            middle(pe, causal, 0)
            last_batch(causal, 0)
            turn(causal, 0, ("post",))
            pe.wait_ge(S["probs_zero"], 1)
            pe.wait_ge(S["zq_ready"], STEPS)
            pe.wait_ge(S["zk_ready"], STEPS)
            pe.wait_ge(S["res_done"], NB)
            credit(pe, per_step="n_done", per_batch="xc_done var_done mlp_done", per_chunk="up_done")
            first_batch(local, 1)

            def start(l):
                pe.wait_ge(S["hid_ready"], 3 * NB * (l + 1))
                pe.wait_ge(S["mlp_res"], NB * (l + 1))

            layers(pe, local, start=start)
            for p in range(PAIRS):
                pe.wait_ge(S["fin_sum"], p + 1)
                for k in range(2 * TT):
                    m = pe.transpose(bank[p][:, k * P:(k + 1) * P], xh[:, 2 * p + k // 2, (k % 2) * P:(k % 2 + 1) * P], ident)
                m.then_inc(S["fin_done"], 1)

        @block.vector
        def _(dve):
            dve.wait_ge(S["const_in"], 16)
            dve.tensor_copy(ident_b[:, :], ident).then_inc(S["masks_ready"], 1)
            dve.tensor_copy(mask_b["causal"][:, :], con("mask_causal")).then_inc(S["masks_ready"], 1)
            dve.tensor_copy(mask_b["local"][:, :], con("mask_local")).then_inc(S["masks_ready"], 1)
            NT = NB * TT
            dve.wait_ge(S["x_in"], 16)
            dve.tensor_reduce(stats[:, 0, :], x_rows[:, :, :], AX_X, ALU.add).then_inc(S["mean"], 1)
            dve.wait_ge(S["mean"], 1)
            dve.tensor_scalar(stats[:, 1, :], stats[:, 0, :], 1.0 / P, None, ALU.mult).then_inc(S["mean"], 1)
            dve.wait_ge(S["mean"], 2)
            dve.tensor_tensor(xn_rows[:, :, :], x_rows[:, :, :], stats[:, 1, :].unsqueeze(2).broadcast_to([P, NT, P]), ALU.subtract).then_inc(S["centred"], 1)
            dve.wait_ge(S["squared"], 1)
            dve.tensor_reduce(stats[:, 1, :], xh[:, :, :].rearrange("p a (t c) -> p (a t) c", c=P), AX_X, ALU.add).then_inc(S["var_sum"], 1)
            dve.wait_ge(S["rstd_row"], 1)
            dve.tensor_tensor(xn_rows[:, :, :], xn_rows[:, :, :], stats[:, 3, :].unsqueeze(2).broadcast_to([P, NT, P]), ALU.mult).then_inc(S["xn_ready"], 1)
            dve.wait_ge(S["zeros_ready"], 2)
            for p in range(PAIRS):
                dve.wait_ge(S["xnt_done"], p + 1)
                src = bank[p][:, :].rearrange("p (a t) -> p a t", a=2)
                dve.tensor_copy(attn[:, 2 * p:2 * p + 2, :], src).then_inc(S["xt_ready"], 1)
                dve.tensor_copy(xs[0:64, 2 * p:2 * p + 2, 0:T], src[0:64]).then_inc(S["xs_ready"], 1)
                dve.tensor_copy(xs[64:P, 2 * p:2 * p + 2, 1:T + 1], src[64:P]).then_inc(S["xs_ready"], 1)

            dve.wait_ge(S["pars_turned"], 1)
            dve.tensor_copy(pars[:, :, :], B_Q[:, 0:NPAR * DEPTH].rearrange("p (j l) -> p j l", j=NPAR)).then_inc(S["pars_ready"], 1)

            def maxima(kind, n, pair):
                for h in (2 * pair, 2 * pair + 1):
                    dve.wait_ge(S["qk_done"], HG * n + h + 1)
                    at = 0
                    for t, (k0, w) in enumerate(SPANS[kind]):
                        m = dve.tensor_reduce(nm[:, h, t:t + 1], B_S[h][:, at:at + w], AX_X, ALU.max, negate=True)
                        at += w
                    m.then_inc(S["nm_ready"], 1)

            def probabilities(kind, n, pair):
                heads = slice(2 * pair, 2 * pair + 2)
                dve.wait_ge(S["exp_done"], HG * n + 2 * pair + 2)
                dve.reciprocal(rrec[:, heads, :], rsum[:, heads, :]).then_inc(S["rrec_ready"], 1)
                dve.wait_ge(S["rrec_ready"], 2 * n + pair + 1)
                for h in (2 * pair, 2 * pair + 1):
                    for t, (k0, w) in enumerate(SPANS[kind]):
                        seen = probs[:, h, t * P + k0:t * P + k0 + w]
                        m = dve.tensor_scalar(seen, seen, rrec[:, h, t:t + 1], None, ALU.mult)
                    m.then_inc(S["pn_ready"], 1)

            def pt_out(kind, n, pair):
                for h in PT_ON_DVE:
                    if h // 2 == pair:
                        dve.wait_ge(S["pt_done"], HG * n + h + 1)
                        after(dve, "pv_done", n)
                        dve.tensor_copy(probs_t[:, h, 0:PT_COLS[kind]], B_S[h][:, 0:PT_COLS[kind]]).then_inc(S["pt_dve"], 1)

            def bound_inverse(n1):
                dve.wait_ge(S["rinv_ready"], n1 + 1)
                dve.tensor_scalar(rinv[:, :, :], rinv[:, :, :], 1e12 / ROOT, None, ALU.min).then_inc(S["inv_norm_ready"], 1)

            def rotate(n1, idx):
                squared, bankx, mark, taken = (("q_square", B_Q, "q_prod", "q_summed"), ("k_square", B_K, "k_prod", "k_summed"))[idx]
                dve.wait_ge(S[squared], n1 + 1)
                dve.wait_ge(S[taken], n1)
                src = bankx[:, :].rearrange("p (a t) -> p a t", a=2)
                dve.tensor_tensor(rot_u[:, idx, :, :], src, tabs[:, 2 * idx, :, :], ALU.mult)
                dve.tensor_tensor(rot_v[:, idx, :, :], src, tabs[:, 2 * idx + 1, :, :], ALU.mult).then_inc(S[mark], 1)

            def hidden(m, banks):
                for c in range(3):
                    dve.wait_ge(S["gelu_done"], 3 * m + c + 1)
                    dve.wait_ge(S["mlp_done"], m)
                    dve.scalar_tensor_tensor(out=hid[0:CW[c], c, :], in0=banks[c][0:CW[c], 0:T], scalar=par[0:CW[c], BA - LG + c:BA - LG + c + 1],
                                             in1=gate[0:CW[c], c, :], op0=ALU.add, op1=ALU.mult).then_inc(S["hid_ready"], 1)

            def residual(m, b, out_bank):
                dve.wait_ge(S["mlp_done"], m + 1)
                for rows, at in ((slice(0, 64), 0), (slice(64, P), 1)):
                    dst = xs[rows, b, at:at + T]
                    a = dve.scalar_tensor_tensor(out=dst, in0=out_bank[rows, 0:T], scalar=par[rows, B2 - LG:B2 - LG + 1], in1=dst, op0=ALU.add, op1=ALU.add)
                a.then_inc(S["mlp_res"], 1)

            def step(kind, ph, b, has, g, odd):
                i = ph * NB + b
                s1, s2, post = ("s1" in has), ("s2" in has), ("post" in has)
                batch = stage1_batch(i, has)
                n, n1 = i * G + g, stage1_batch(i, has) * G + g
                mlp, m = "mlp" in has, ph * NB
                if s1 and g == 0:
                    after(dve, "v_done", batch * G)
                    if kind == "causal":
                        dve.tensor_copy(latent[:, :], xh[:, ds(b + 1, 1), :].rearrange("p a t -> p (a t)")).then_inc(S["xin_ready"], 1)
                    else:
                        src = xs[:, ds(0 if "turn" in has else b + 1, 1), 0:T].rearrange("p a t -> p (a t)")
                        dve.tensor_copy(xin[:, :], src).then_inc(S["xin_ready"], 1)
                late = late_pair(g, has)
                if s2:
                    maxima(kind, n, 0)
                if late:
                    pt_out(kind, n - 1, 1)
                if mlp and s2 and g and AMID[g - 1] is not None:
                    residual(m + AMID[g - 1], AMID[g - 1], MLP_LATE[1])
                if post and g == 1:
                    dve.wait_ge(S["wo_done"], i)
                    if kind == "causal":
                        dve.tensor_copy(attn[:, ds(b - 1, 1), :].rearrange("p a t -> p (a t)"), B_Q[:, 0:T]).then_inc(S["res_done"], 1)
                    else:
                        lo = xs[0:64, ds(b - 1, 1), 0:T].rearrange("p a t -> p (a t)")
                        hi = xs[64:P, ds(b - 1, 1), 1:T + 1].rearrange("p a t -> p (a t)")
                        dve.tensor_tensor(lo, B_Q[0:64, 0:T], lo, ALU.add)
                        dve.tensor_tensor(hi, B_Q[64:P, 0:T], hi, ALU.add).then_inc(S["res_done"], 1)
                if post and kind == "local" and g == 2:
                    dve.wait_ge(S["xc_done"], i)
                    dve.tensor_copy(xc[:, :], B_Q[:, 0:T]).then_inc(S["xc_ready"], 1)
                if mlp and not s2 and g == 0:
                    hidden(m + NB - 2, MLP_TURN[0])
                if s2:
                    probabilities(kind, n, 0)
                    maxima(kind, n, 1)
                    pt_out(kind, n, 0)
                if s1 and kind == "causal":
                    dve.wait_ge(S["k_done"], n1 + 1)
                    after(dve, "qk_done", HG * (n1 + 1 - G))
                    dve.tensor_copy(zqk[:, g, 1, :, :], B_K[:, :].rearrange("p (a t) -> p a t", a=2)).then_inc(S["zk_ready"], 1)
                if kind == "local" and norms_due(g, has):
                    bound_inverse(n1 - 1)
                if s1 and kind == "local":
                    rotate(n1, 1)
                if mlp and s2:
                    hidden(m + EARLY[g], MLP_LATE[0])
                if mlp and s2:
                    residual(m + EARLY[g], EARLY[g], MLP_LATE[1])
                    if AMID[g] is not None:
                        hidden(m + AMID[g], MLP_LATE[0])
                if s2:
                    probabilities(kind, n, 1)
                if s1 and kind == "local":
                    rotate(n1, 0)
                if post and kind == "local" and g == 3:
                    dve.wait_ge(S["rstd_ready"], i)
                    dve.tensor_tensor(xc[:, :], xc[:, :], rstd[:, :], ALU.mult).then_inc(S["xh_raw"], 1)
                    dve.wait_ge(S["xh_raw"], i)
                    dve.tensor_scalar(xh[:, ds(b - 1, 1), :].rearrange("p a t -> p (a t)"), xc[:, :], par[:, 0:1], par[:, LB - LG:LB - LG + 1],
                                      ALU.mult, ALU.add).then_inc(S["xh_ready"], 1)
                if mlp and not s2 and g == 0:
                    residual(m + NB - 2, NB - 2, MLP_TURN[1])
                if mlp and not s2 and g == G - 1:
                    hidden(m + NB - 1, MLP_TURN[0])
                    residual(m + NB - 1, NB - 1, MLP_TURN[1])

            def rotary_tables(l):
                dve.wait_ge(S["q_prod"], (l + 1) * STEPS)
                dve.wait_ge(S["k_prod"], (l + 1) * STEPS)
                dve.wait_ge(S["tabs_ready"], l)
                dve.tensor_copy(par_rot[:, :], pars[:, 0:LG, ds(l, 1)].rearrange("p n a -> p (n a)")).then_inc(S["par_rot_ready"], 1)
                dve.wait_ge(S["par_rot_ready"], l + 1)
                for k, (c1, sign) in enumerate(((Q1, 1), (Q1, -1), (K1, 1), (K1, -1))):
                    for half in range(2):
                        m = dve.tensor_scalar(tabs[:, k, half, :], con("rot")[:, k * T:(k + 1) * T], par_rot[:, c1 + half:c1 + half + 1],
                                              float(sign if half else 1), ALU.mult, ALU.mult)
                m.then_inc(S["tabs_ready"], 1)
                dve.wait_ge(S["tabs_ready"], l + 1)

            def start(l):
                dve.wait_ge(S["mlp_res"], (l + 1) * NB)
                dve.wait_ge(S["gelu_done"], 3 * (l + 1) * NB)
                dve.tensor_copy(par[:, :], pars[:, LG:NPAR, ds(l, 1)].rearrange("p n a -> p (n a)")).then_inc(S["par_ready"], 1)
                dve.wait_ge(S["par_ready"], l + 1)

            causal = lambda ph, b, has, g, odd: step("causal", ph, b, has, g, odd)
            local = lambda ph, b, has, g, odd: step("local", ph, b, has, g, odd)
            dve.wait_ge(S["latent_ready"], PAIRS)
            first_batch(causal, 0)
            middle(dve, causal, 0)
            last_batch(causal, 0)
            turn(causal, 0, ("post",))
            credit(dve, per_step="q_prod k_prod inv_norm_ready", per_batch="xc_ready xh_raw xh_ready mlp_res", per_chunk="hid_ready")
            rotary_tables(0)
            first_batch(local, 1)
            layers(dve, local, start=start, between=lambda l: rotary_tables(l + 1))
            dve.wait_ge(S["mlp_res"], (DEPTH + 1) * NB)
            for p in range(PAIRS):
                for rows, at in ((slice(0, 64), 0), (slice(64, P), 1)):
                    a = dve.tensor_tensor(xh[rows, 2 * p:2 * p + 2, :], xs[rows, 2 * p:2 * p + 2, at:at + T], attn[rows, 2 * p:2 * p + 2, :], ALU.add)
                a.then_inc(S["fin_sum"], 1)
            for p in range(PAIRS):
                dve.wait_ge(S["fin_done"], p + 1)
                tiles = slice(2 * TT * p, 2 * TT * (p + 1))
                dve.tensor_tensor(xn_rows[:, tiles, :], bank[p][:, :].rearrange("p (k c) -> p k c", c=P), x_rows[:, tiles, :], ALU.add).then_inc(S["rows_ready"], 1)


_INS = ["L0_attn_x", "L0_attn_w_kv_down", "L0_attn_w_kv_up", "L0_attn_w_q", "L0_attn_w_out", "L0_ffn_Wqkv",
        "L0_ffn_q_scale", "L0_ffn_k_scale", "L0_ffn_Wo", "L0_ffn_ln_g", "L0_ffn_ln_b", "L0_ffn_W1", "L0_ffn_b1",
        "L0_ffn_W2", "L0_ffn_b2"]


def kernel(**inputs):
    import concourse.bacc as bacc
    from concourse.bass_utils import run_bass_kernel_spmd

    nc = bacc.Bacc("TRN2", target_bir_lowering=False, num_devices=1)
    arrays = {f"in_{name}": np.ascontiguousarray(inputs[name]) for name in _INS}
    arrays["in_constants"] = constants()
    for name, ranges in (("L0_ffn_Wqkv", 2),):
        a = arrays[f"in_{name}"].copy()
        for k in range(ranges):
            part = a[..., k * HD:(k + 1) * HD].reshape(*a.shape[:-1], G, HG, 2, D // 2)
            a[..., k * HD:(k + 1) * HD] = np.moveaxis(part, -2, -3).reshape(*a.shape[:-1], HD)
        arrays[f"in_{name}"] = a
    args = [nc.dram_tensor(n, a.shape, F32, kind="ExternalInput").ap() for n, a in arrays.items()]
    out = nc.dram_tensor("out_0", (NB, T, P), F32, kind="ExternalOutput").ap()
    build(nc, *args, out)
    r = run_bass_kernel_spmd(nc, [arrays], core_ids=[0])
    return r.results[0]["out_0"]
```

```python
from contextlib import ExitStack

import numpy as np

import concourse.bass as bass
from concourse import mybir

F32 = mybir.dt.float32
BF16 = mybir.dt.bfloat16
F32R = mybir.dt.float32r
ALU = mybir.AluOpType
ACT = mybir.ActivationFunctionType
AX_X = mybir.AxisListType.X
ds = bass.ds

P = 128
NB, T = 8, 256
TT = T // P
DEPTH = 6
H, D = 16, 64
G, HG = 4, 4
HD = H * D
GW = HG * D
STEPS = NB * G
WIN = 32
LN_EXP = "natural_log_exp_and_others"
INNER = P * 4 * 2 // 3
CW = [P, P, INNER - 2 * P]
PAIRS = NB // 2
N_SMALL = 4 * HG + 6 + 3
QK_SCALE = 8.0
NBIG = -1e30
LNS = 2.0 ** 30
ROOT = 2.0 ** 15
EPS = 1e-5
SPANS = {"causal": [(0, P), (0, 2 * P)], "local": [(0, P), (P - WIN, P + WIN)]}
PT_COLS = {"causal": 3 * P, "local": 2 * P + WIN}
PT_ON_DVE, PT_ON_ACT = (1, 3), (0, 2)
Q1, Q2, K1, K2, LG, LB, B2, BA, BG, NPAR = 0, 1, 2, 3, 4, 5, 6, 7, 10, 13

CONST = {}
_at = 0
for _name, _n in (("ident", P), ("mask_causal", 3 * P), ("mask_local", 2 * P + WIN), ("blk", P),
                  ("center", P), ("avg", P), ("rot", 4 * T)):
    CONST[_name] = (_at, _n)
    _at += _n
NCONST = _at


def constants():
    c = np.zeros((P, NCONST), np.float32)

    def put(name, a):
        at, n = CONST[name]
        c[:, at:at + n] = a

    i = np.arange(P)[:, None]
    put("ident", np.eye(P))
    masks = {}
    for kind in SPANS:
        parts = []
        for t, (k0, w) in enumerate(SPANS[kind]):
            q, k = i + P * t, k0 + np.arange(w)[None, :]
            ok = k <= q
            if kind == "local":
                ok = ok & (k >= q - WIN)
            parts.append(np.where(ok, 0.0, NBIG))
        masks[kind] = np.concatenate(parts, 1)
    put("mask_causal", masks["causal"])
    put("mask_local", masks["local"])
    put("blk", i // 32 == np.arange(P)[None, :] // 32)
    put("avg", np.full((P, P), 1.0 / P))
    put("center", np.eye(P) - 1.0 / P)
    half = np.arange(0, D, 2, dtype=np.float32)
    inv = (1.0 / np.float32(10000.0) ** (half / np.float32(D))).astype(np.float32)
    pos = np.arange(T, dtype=np.float32)
    freqs = (pos[None, :] * inv[:, None]).astype(np.float32).astype(np.float64)
    base = ((half + np.float32(0.4 * D)) / np.float32(1.4 * D)).astype(np.float64)
    scale = base[:, None] ** ((pos[None, :] - T // 2) / (WIN // 2)).astype(np.float64)
    cos, sin = np.cos(freqs), np.sin(freqs)
    rot = np.concatenate([cos * scale * (QK_SCALE * ROOT), sin * scale * (QK_SCALE * ROOT), cos / scale * ROOT, sin / scale * ROOT], 1)
    put("rot", np.tile(rot, (HG, 1)))
    return c


def build(nc, x, w_kv_down, w_kv_up, w_q, w_out, Wqkv, q_scale, k_scale, Wo, ln_g, ln_b, W1, b1, W2, b2, const, out):
    with ExitStack() as ctx:
        def sb(name, shape, dt=F32):
            return ctx.enter_context(nc.sbuf_tensor(name, shape, dt))

        def sem(name):
            return ctx.enter_context(nc.semaphore(name))

        consts = sb("consts", [P, NCONST])

        def con(name):
            at, n = CONST[name]
            return consts[:, at:at + n]

        ident = con("ident")
        ident_b = sb("ident_b", [P, P], BF16)
        mask_b = {"causal": sb("mask_causal_b", [P, 3 * P], BF16), "local": sb("mask_local_b", [P, 2 * P + WIN], BF16)}
        stats = sb("stats", [P, 4, NB * TT])
        xs = sb("xs", [P, NB, T + 1])
        attn = sb("attn", [P, NB, T])
        xh = sb("xh", [P, NB, T])
        x_high = sb("x_high", [P, T], F32R)
        x_low = sb("x_low", [P, T], F32R)
        latent = sb("latent", [P, T])
        wdown = sb("wdown", [P, P])
        w_qkv = sb("w_qkv", [P, 3, HD])
        w_high = sb("w_high", [P, 3, HD], F32R)
        w_low = sb("w_low", [P, 3, HD], F32R)
        wq, wk, wv = w_qkv[:, 0, :], w_qkv[:, 1, :], w_qkv[:, 2, :]
        wo = sb("wo", [P, HD // P, P])
        w1 = sb("w1", [P, 2 * INNER])
        w2 = sb("w2", [P, 3, P])
        par_rows = sb("par_rows", [NPAR * DEPTH, P])
        pars = sb("pars", [P, NPAR, DEPTH])
        par_rot = sb("par_rot", [P, LG])
        par = sb("par", [P, NPAR - LG])
        tabs = sb("tabs", [P, 4, 2, T])
        rot_u = sb("rot_u", [P, 2, 2, T])
        rot_v = sb("rot_v", [P, 2, 2, T])
        sq = sb("sq", [P, 2, 2, T])
        sqs = sb("sqs", [P, 2, T])
        ln_n = sb("ln_n", [P, 2, T])
        rinv = sb("rinv", [P, 2, T])
        z_raw = sb("z_raw", [P, 2, 2, T])
        z_norm = sb("z_norm", [P, 2, 2, 2, T])
        zqk = sb("zqk", [P, G, 2, 2, T])
        v_sb = sb("v_sb", [P, 2, TT, HD])
        nm = sb("nm", [P, HG, TT])
        x_rows = zqk[:, 0:2, :, :, :].rearrange("p g a b t -> p (g a b t)").rearrange("p (n c) -> p n c", c=P)
        xn_rows = v_sb[:, 0, :, :].rearrange("p a t -> p (a t)").rearrange("p (n c) -> p n c", c=P)
        probs = sb("probs", [P, HG, 3 * P])
        probs_t = sb("probs_t", [P, HG, 3 * P])
        rsum = sb("rsum", [P, HG, TT])
        rrec = sb("rrec", [P, HG, TT])
        yt = sb("yt", [P, HD // P, T])
        xc = sb("xc", [P, T])
        xc2 = sb("xc2", [P, T])
        ln_v = sb("ln_v", [P, T])
        rstd = sb("rstd", [P, T])
        gate = sb("gate", [P, 3, T])
        hid = sb("hid", [P, 3, T])
        tiny = sb("tiny", [P, 2])

        bank = [ctx.enter_context(nc.psum_tensor(f"bank{i}", [P, 512], F32)) for i in range(8)]
        B_S, B_Q, B_K, B_Y, B_N = bank[:4], bank[4], bank[5], bank[6], bank[7]

        names = """const_in x_in small_in wkv_down_in wqk_in wv_in wo_in w1_in w2_in out_dma
            tiny_ready zeros_ready masks_ready mean centred squared var_sum rstd_ln rstd_row xn_ready xnt_done xt_ready xs_ready
            pars_turned pars_ready probs_zero par_rot_ready par_ready tabs_ready xin_ready x_high_ready weights_met w_high_ready w_split down_done latent_ready
            q_done k_done q_prod k_prod q_square k_square sums_ready zq_ready zk_ready k_summed q_summed inv_norm_ready zn_ready n_done ln_done rinv_ready
            z_in0 z_in1 z_in2 z_in3 v_done v_ready qk_done nm_ready exp_done rrec_ready pn_ready pt_done pt_dve pt_act pv_done
            yt_ready wo_done res_done xc_done xc_ready xc_squared var_done ln_var rstd_ready xh_raw xh_ready
            up_done gelu_done hid_ready mlp_done mlp_res fin_sum fin_done rows_ready""".split()
        S = {n: sem(n) for n in names}

        def late_banks(b):
            return ((B_N, B_K, B_N), (B_K, B_N, B_K))[b % 2]

        TURN_BANKS = (bank[0], bank[1], bank[2])

        def post_bank(has):
            return bank[3] if "turn" in has else B_Q

        BEGUN, WHOLE = (None, 1, 3, 5), (0, 2, 4, None)

        def after(eng, name, value):
            if not (isinstance(value, int) and value <= 0):
                eng.wait_ge(S[name], value)

        def credit(eng, per_step="", per_batch="", per_chunk=""):
            for name in per_step.split():
                eng.sem_inc(S[name], STEPS)
            for name in per_batch.split():
                eng.sem_inc(S[name], NB)
            for name in per_chunk.split():
                eng.sem_inc(S[name], 3 * NB)

        def z_landed(batches):
            return 16 * 2 * HG * batches

        def stage1_batch(i, has):
            return i if "turn" in has else i + 1

        def stage1_odd(odd, has):
            return odd if "turn" in has else 1 - odd

        def norms_due(g, has):
            return "s1" in has if g else "s2" in has

        def late_pair(g, has):
            return "s2" in has if g else "post" in has

        def first_batch(step, ph):
            for g in range(G):
                step(ph, -1, ("s1",), g, 1)

        def middle(eng, step, ph):
            for g in range(G):
                step(ph, 0, ("s1", "s2"), g, 0)
            with eng.Fori(0, NB // 2 - 1) as r:
                for odd in (1, 0):
                    for g in range(G):
                        step(ph, 2 * r + 2 - odd, ("s1", "s2", "post"), g, odd)

        def last_batch(step, ph, has=("s2", "post"), between=None, l=None):
            for g in range(G):
                step(ph, NB - 1, has, g, 1)
                if between and g == 0:
                    between(l)

        def turn(step, ph, has):
            for g in range(G):
                step(ph, NB, has, g, 0)

        def layers(eng, step, start=None, between=None):
            def layer(l, has):
                if start:
                    start(l)
                middle(eng, step, l + 1)
                last_batch(step, l + 1, ("s2", "post", "mlp"), between if "s1" in has else None, l)
                turn(step, l + 1, has)

            with eng.Fori(0, DEPTH - 1) as l:
                layer(l, ("s1", "post", "mlp", "turn"))
            layer(DEPTH - 1, ("post", "mlp", "turn"))

        block = ctx.enter_context(nc.Block())

        @block.sync
        def _(sp):
            sp.dma_start(consts[:, :], const).then_inc(S["const_in"], 16)
            sp.dma_start(x_rows[:, :, :], x.rearrange("b (t p) c -> p (b t) c", p=P)).then_inc(S["x_in"], 16)
            sp.dma_start(wdown[:, :], w_kv_down).then_inc(S["wkv_down_in"], 16)
            sp.dma_start(wq, w_q).then_inc(S["wqk_in"], 16)
            sp.dma_start(wk, w_kv_up[:, 0:HD]).then_inc(S["wqk_in"], 16)
            sp.dma_start(wv, w_kv_up[:, HD:2 * HD]).then_inc(S["wv_in"], 16)
            sp.dma_start(wo[:, :, :], w_out.rearrange("(c p) n -> p c n", p=P)).then_inc(S["wo_in"], 16)
            sp.dma_start(w1[:, :], W1[0, :, :]).then_inc(S["w1_in"], 16)
            sp.dma_start(w2[:, 0:2, :], W2[0, 0:2 * P, :].rearrange("(c p) n -> p c n", p=P)).then_inc(S["w2_in"], 16)
            sp.dma_start(w2[0:CW[2], 2, :], W2[0, 2 * P:INNER, :]).then_inc(S["w2_in"], 16)
            n_small = 0

            def small(dst, src):
                nonlocal n_small
                sp.dma_start(dst, src).then_inc(S["small_in"], 16)
                n_small += 1

            def param_rows(j):
                return par_rows[j * DEPTH:(j + 1) * DEPTH]

            sp.wait_ge(S["zeros_ready"], 2)
            for hh in range(HG):
                for half in range(2):
                    cols, own = slice(32 * hh, 32 * hh + 32), slice(32 * half, 32 * half + 32)
                    small(param_rows(Q1 + half)[:, cols], q_scale[:, own])
                    small(param_rows(K1 + half)[:, cols], k_scale[:, own])
            for c in range(3):
                for at, j in ((0, BA), (INNER, BG)):
                    small(param_rows(j + c)[:, 0:CW[c]], b1[:, at + c * P:at + c * P + CW[c]])
            for src, j in ((ln_g, LG), (ln_b, LB), (b2, B2)):
                small(param_rows(j), src)
            assert n_small == N_SMALL

            def qkv_weights(l):
                sp.wait_ge(S["v_done"], (l + 1) * STEPS)
                row = Wqkv[ds(l, 1), :, :].rearrange("a p n -> (a p) n")
                sp.dma_start(wq, row[:, 0:HD]).then_inc(S["wqk_in"], 16)
                sp.dma_start(wk, row[:, HD:2 * HD]).then_inc(S["wqk_in"], 16)
                sp.dma_start(wv, row[:, 2 * HD:3 * HD]).then_inc(S["wv_in"], 16)

            def out_weights(l):
                sp.wait_ge(S["wo_done"], (l + 1) * NB + 1)
                sp.dma_start(wo[:, :, :], Wo[ds(l, 1), :, :].rearrange("a (c p) n -> p (a c) n", p=P)).then_inc(S["wo_in"], 16)

            def mlp_weights(l):
                sp.wait_ge(S["mlp_done"], (l + 1) * NB)
                sp.dma_start(w1[:, :], W1[ds(l, 1), :, :].rearrange("a p n -> (a p) n")).then_inc(S["w1_in"], 16)
                row = W2[ds(l, 1), :, :].rearrange("a p n -> (a p) n")
                sp.dma_start(w2[:, 0:2, :], row[0:2 * P, :].rearrange("(c p) n -> p c n", p=P)).then_inc(S["w2_in"], 16)
                sp.dma_start(w2[0:CW[2], 2, :], row[2 * P:INNER, :]).then_inc(S["w2_in"], 16)

            def step(ph, b, has, g, odd):
                i = ph * NB + b
                if "s1" not in has:
                    return
                n1 = stage1_batch(i, has) * G + g
                if "turn" in has and g == 1:
                    out_weights(ph)
                if "turn" in has and g == G - 1:
                    mlp_weights(ph)
                sp.wait_ge(S["zn_ready"], n1 + 1)
                for h in range(HG):
                    for half in range(2):
                        to = 64 * (h % 2) + 32 * half
                        sp.dma_start(zqk[to:to + 32, g, :, h // 2, :], z_norm[32 * h:32 * h + 32, g % 2, :, half, :]).then_inc(S[f"z_in{g}"], 16)

            qkv_weights(0)
            out_weights(0)
            first_batch(step, 1)
            layers(sp, step, between=lambda l: qkv_weights(l + 1))
            sp.wait_ge(S["qk_done"], HG * (DEPTH + 1) * STEPS)
            sp.dma_start(x_rows[:, :, :], x.rearrange("b (t p) c -> p (b t) c", p=P)).then_inc(S["x_in"], 16)
            for p in range(PAIRS):
                sp.wait_ge(S["rows_ready"], p + 1)
                b0 = 2 * p
                sp.dma_start(out[b0:b0 + 2, :, :].rearrange("b (t p) c -> p (b t) c", p=P),
                             xn_rows[:, TT * b0:TT * b0 + 2 * TT, :]).then_inc(S["out_dma"], 16)
            sp.wait_ge(S["out_dma"], 16 * PAIRS)

        @block.gpsimd
        def _(pool):
            pool.memset(tiny[:, 0:1], 2.0 ** -64).then_inc(S["tiny_ready"], 1)
            pool.wait_ge(S["tiny_ready"], 1)
            pool.memset(tiny[:, 1:2], EPS).then_inc(S["tiny_ready"], 1)
            pool.wait_ge(S["tiny_ready"], 2)
            pool.memset(xs[64:P, :, 0:1], 0.0).then_inc(S["zeros_ready"], 1)
            pool.wait_ge(S["zeros_ready"], 1)
            pool.memset(par_rows[:, :], 0.0).then_inc(S["zeros_ready"], 1)

            def normalise(j, g, idx):
                n1 = j * G + g
                if idx == 1:
                    pool.wait_ge(S["inv_norm_ready"], n1 + 1)
                    after(pool, f"z_in{(g - 2) % G}", z_landed(j - NB + (1 if g >= 2 else 0)))
                pool.wait_ge(S[("q_summed", "k_summed")[idx]], n1 + 1)
                m = pool.tensor_tensor(z_norm[:, g % 2, idx, :, :], rinv[:, idx, :].unsqueeze(1).broadcast_to([P, 2, T]), z_raw[:, idx, :, :], ALU.mult)
                if idx == 0:
                    m.then_inc(S["zn_ready"], 1)

            def step(ph, b, has, g, odd):
                i = ph * NB + b
                batch = stage1_batch(i, has)
                n1 = batch * G + g
                if "s1" in has:
                    pool.wait_ge(S["k_square"], n1 + 1)
                    pool.wait_ge(S["q_square"], n1 + 1)
                    pool.wait_ge(S["n_done"], n1)
                    pool.tensor_tensor(sqs[:, :, :], sq[:, :, 0, :], sq[:, :, 1, :], ALU.add).then_inc(S["sums_ready"], 1)
                if "s2" in has and norms_due(g, has):
                    normalise(batch if g else batch - 1, (g - 1) % G, 1)
                if "s2" in has and norms_due(g, has):
                    normalise(batch if g else batch - 1, (g - 1) % G, 0)
                if "s1" in has:
                    pool.wait_ge(S["zn_ready"], n1)
                    for idx, prod, mark in ((1, "k_prod", "k_summed"), (0, "q_prod", "q_summed")):
                        pool.wait_ge(S[prod], n1 + 1)
                        for half in range(2):
                            a = pool.tensor_tensor(z_raw[:, idx, half, :], rot_u[:, idx, half, :], rot_v[:, idx, 1 - half, :], ALU.add)
                        a.then_inc(S[mark], 1)

            pool.wait_ge(S["pt_done"], HG * STEPS)
            pool.memset(probs[:, :, P:2 * P - WIN], 0.0).then_inc(S["probs_zero"], 1)
            credit(pool, per_step="k_summed q_summed sums_ready zn_ready")
            def split_weights(l):
                pool.wait_ge(S["wqk_in"], 32 * (l + 2))
                pool.wait_ge(S["wv_in"], 16 * (l + 2))
                pool.sem_inc(S["weights_met"], 1)
                for k in range(3):
                    a = pool.tensor_copy(w_high[:, k, :], w_qkv[:, k, :])
                a.then_inc(S["w_high_ready"], 1)
                pool.wait_ge(S["w_high_ready"], l + 1)
                for k in range(3):
                    a = pool.tensor_tensor(w_low[:, k, :], w_qkv[:, k, :], w_high[:, k, :].bitcast(F32), ALU.subtract)
                a.then_inc(S["w_split"], 1)

            split_weights(0)
            first_batch(step, 1)
            layers(pool, step, between=lambda l: split_weights(l + 1))

        @block.scalar
        def _(act):
            act.preload_act_table_set(LN_EXP)
            flat = xn_rows[:, :, :].rearrange("p a c -> p (a c)")
            act.wait_ge(S["centred"], 1)
            act.activation(xh[:, :, :].rearrange("p a c -> p (a c)"), flat, ACT.Square).then_inc(S["squared"], 1)
            act.wait_ge(S["tiny_ready"], 2)
            act.wait_ge(S["var_sum"], 1)
            act.activation(stats[:, 2, :], stats[:, 1, :], ACT.Ln, bias=tiny[:, 1:2], scale=1.0 / P).then_inc(S["rstd_ln"], 1)
            act.wait_ge(S["rstd_ln"], 1)
            act.activation(stats[:, 3, :], stats[:, 2, :], ACT.Exp, scale=-0.5).then_inc(S["rstd_row"], 1)

            for p in range(PAIRS):
                act.wait_ge(S["down_done"], p + 1)
                act.wait_ge(S["var_sum"], 1)
                act.activation(xh[:, 2 * p:2 * p + 2, :], bank[p][:, :].rearrange("p (a t) -> p a t", a=2), ACT.Copy).then_inc(S["latent_ready"], 1)

            def exps(kind, n, pair):
                for h in (2 * pair, 2 * pair + 1):
                    act.wait_ge(S["nm_ready"], HG * n + h + 1)
                    at = 0
                    for t, (k0, w) in enumerate(SPANS[kind]):
                        a = act.activation(probs[:, h, t * P + k0:t * P + k0 + w], B_S[h][:, at:at + w], ACT.Exp,
                                           bias=nm[:, h, t:t + 1], accum_out=rsum[:, h, t:t + 1])
                        at += w
                    a.then_inc(S["exp_done"], 1)

            def pt_out(kind, n, pair):
                for h in PT_ON_ACT:
                    if h // 2 == pair:
                        act.wait_ge(S["pt_done"], HG * n + h + 1)
                        after(act, "pv_done", n)
                        act.activation(probs_t[:, h, 0:PT_COLS[kind]], B_S[h][:, 0:PT_COLS[kind]], ACT.Copy).then_inc(S["pt_act"], 1)

            def yt_out(i, g):
                n = i * G + g
                act.wait_ge(S["pv_done"], n + 1)
                act.wait_ge(S["wo_done"], i + 1)
                act.activation(yt[:, 2 * g:2 * g + 2, :], B_Y[:, :].rearrange("p (c t) -> p c t", c=2), ACT.Copy).then_inc(S["yt_ready"], 1)

            def v_out(n1, g, odd):
                act.wait_ge(S["v_done"], n1 + 1)
                after(act, "pv_done", n1 - G)
                act.activation(v_sb[:, odd, :, g * GW:(g + 1) * GW], B_N[:, :].rearrange("p (t n) -> p t n", t=TT), ACT.Copy).then_inc(S["v_ready"], 1)

            def squares(n1, which):
                done, bankx, idx, mark = (("k_done", B_K, 1, "k_square"), ("q_done", B_Q, 0, "q_square"))[which]
                act.wait_ge(S[done], n1 + 1)
                act.wait_ge(S["sums_ready"], n1)
                act.activation(sq[:, idx, :, :], bankx[:, :].rearrange("p (a t) -> p a t", a=2), ACT.Square).then_inc(S[mark], 1)

            def gelus(m, banks):
                for c in range(3):
                    act.wait_ge(S["up_done"], 3 * m + c + 1)
                    act.wait_ge(S["hid_ready"], 3 * (m - 1) + c + 1)
                    act.activation(gate[0:CW[c], c, :], banks[c][0:CW[c], T:2 * T], ACT.Gelu, bias=par[0:CW[c], BG - LG + c:BG - LG + c + 1]).then_inc(S["gelu_done"], 1)

            def step(kind, ph, b, has, g, odd):
                i = ph * NB + b
                s1, s2, post = ("s1" in has), ("s2" in has), ("post" in has)
                n, n1 = i * G + g, stage1_batch(i, has) * G + g
                mlp, m, late = "mlp" in has, ph * NB, late_pair(g, has)
                if norms_due(g, has):
                    v_out(n1 - 1, (g - 1) % G, stage1_odd(odd, has) if g else 1 - stage1_odd(odd, has))
                if late:
                    pt_out(kind, n - 1, 1)
                whole = WHOLE[g] if mlp and s2 else None
                if s2:
                    exps(kind, n, 0)
                if s1 and kind == "local":
                    squares(n1, 0)
                if late:
                    yt_out(i if g else i - 1, (g - 1) % G)
                if s2 and kind == "local" and norms_due(g, has):
                    act.wait_ge(S["n_done"], n1)
                    act.activation(ln_n[:, :, :], B_N[:, :].rearrange("p (a t) -> p a t", a=2), ACT.Ln, bias=tiny[:, 0:1], scale=LNS).then_inc(S["ln_done"], 1)
                    act.wait_ge(S["ln_done"], n1)
                    act.wait_ge(S["zn_ready"], n1 - 1)
                    act.activation(rinv[:, :, :], ln_n[:, :, :], ACT.Exp, scale=-0.5).then_inc(S["rinv_ready"], 1)
                if post and kind == "local" and g == 2:
                    act.wait_ge(S["xc_ready"], i)
                    after(act, "var_done", i - 1)
                    act.activation(xc2[:, :], xc[:, :], ACT.Square).then_inc(S["xc_squared"], 1)
                if post and kind == "local" and g == 3:
                    act.wait_ge(S["var_done"], i)
                    act.activation(ln_v[:, :], post_bank(has)[:, 0:T], ACT.Ln, bias=tiny[:, 1:2]).then_inc(S["ln_var"], 1)
                    act.wait_ge(S["ln_var"], i)
                    after(act, "xh_raw", i - 1)
                    act.activation(rstd[:, :], ln_v[:, :], ACT.Exp, scale=-0.5).then_inc(S["rstd_ready"], 1)
                if mlp and not s2 and g == 0:
                    act.preload_act_table(ACT.Gelu)
                    gelus(m + NB - 2, TURN_BANKS)
                    act.preload_act_table_set(LN_EXP)
                if s2:
                    pt_out(kind, n, 0)
                if s2:
                    exps(kind, n, 1)
                if whole is not None:
                    act.preload_act_table(ACT.Gelu)
                    gelus(m + whole, late_banks(whole))
                    gelus(m + BEGUN[g + 1], late_banks(BEGUN[g + 1]))
                    act.preload_act_table_set(LN_EXP)
                if s1 and kind == "causal":
                    act.wait_ge(S["q_done"], n1 + 1)
                    after(act, "qk_done", HG * (n1 + 1 - G))
                    act.activation(zqk[:, g, 0, :, :], B_Q[:, :].rearrange("p (a t) -> p a t", a=2), ACT.Copy, scale=D ** -0.5).then_inc(S["zq_ready"], 1)
                if s1 and kind == "local":
                    squares(n1, 1)
                if not s2 and kind == "local" and norms_due(g, has):
                    act.wait_ge(S["n_done"], n1)
                    act.activation(ln_n[:, :, :], B_N[:, :].rearrange("p (a t) -> p a t", a=2), ACT.Ln, bias=tiny[:, 0:1], scale=LNS).then_inc(S["ln_done"], 1)
                    act.wait_ge(S["ln_done"], n1)
                    act.wait_ge(S["zn_ready"], n1 - 1)
                    act.activation(rinv[:, :, :], ln_n[:, :, :], ACT.Exp, scale=-0.5).then_inc(S["rinv_ready"], 1)
                if post and kind == "local" and g == 3:
                    act.wait_ge(S["xh_raw"], i)
                    act.activation(xh[:, ds(b - 1, 1), :].rearrange("p a t -> p (a t)"), xc[:, :], ACT.Identity,
                                   bias=par[:, LB - LG:LB - LG + 1], scale=par[:, 0:1]).then_inc(S["xh_ready"], 1)
                if mlp and not s2 and g == G - 1:
                    act.preload_act_table(ACT.Gelu)
                    gelus(m + NB - 1, TURN_BANKS)
                    act.preload_act_table_set(LN_EXP)

            causal = lambda ph, b, has, g, odd: step("causal", ph, b, has, g, odd)
            local = lambda ph, b, has, g, odd: step("local", ph, b, has, g, odd)
            first_batch(causal, 0)
            middle(act, causal, 0)
            last_batch(causal, 0)
            turn(causal, 0, ("post",))
            credit(act, per_step="q_square k_square ln_done rinv_ready", per_batch="xc_squared ln_var rstd_ready xh_ready", per_chunk="gelu_done")
            act.preload_act_table_set(LN_EXP)
            first_batch(local, 1)
            layers(act, local)

        @block.tensor
        def _(pe):
            pe.sem_inc(S["wo_done"], 1)
            pe.wait_ge(S["const_in"], 16)
            pe.wait_ge(S["masks_ready"], 3)
            pe.wait_ge(S["xn_ready"], 1)
            for p in range(PAIRS):
                for k in range(2 * TT):
                    m = pe.transpose(bank[p][:, k * P:(k + 1) * P], xn_rows[:, 2 * TT * p + k, :], ident)
                m.then_inc(S["xnt_done"], 1)
            pe.wait_ge(S["wkv_down_in"], 16)
            for p in range(PAIRS):
                pe.wait_ge(S["xt_ready"], p + 1)
                pe.wait_ge(S["xs_ready"], 2 * p + 2)
                pe.matmul(bank[p][:, :], wdown[:, :], attn[:, 2 * p:2 * p + 2, :].rearrange("p a t -> p (a t)"), start=True, stop=True).then_inc(S["down_done"], 1)
            pe.wait_ge(S["small_in"], 16 * N_SMALL)
            pe.transpose(B_Q[:, 0:NPAR * DEPTH], par_rows[:, :], ident[0:NPAR * DEPTH, 0:NPAR * DEPTH]).then_inc(S["pars_turned"], 1)
            pe.wait_ge(S["pars_ready"], 1)
            pe.wait_ge(S["latent_ready"], PAIRS)

            def pt_taken(n, h):
                name, heads = ("pt_dve", PT_ON_DVE) if h in PT_ON_DVE else ("pt_act", PT_ON_ACT)
                after(pe, name, len(heads) * n + heads.index(h) + 1)

            def scores(kind, i, g, pair):
                n = i * G + g
                if pair == 0:
                    if kind == "causal":
                        pe.wait_ge(S["zq_ready"], n + 1)
                        pe.wait_ge(S["zk_ready"], n + 1)
                    else:
                        pe.wait_ge(S[f"z_in{g}"], z_landed(i - NB + 1))
                spans = SPANS[kind]
                w_all = sum(w for _, w in spans)
                heads = (2 * pair, 2 * pair + 1)
                for h in heads:
                    pt_taken(n - 1, h)
                    pe.matmul(B_S[h][:, 0:w_all], ident_b[:, :], mask_b[kind][:, :], start=True, stop=True)
                at = 0
                for t, (k0, w) in enumerate(spans):
                    for h in heads:
                        r = slice(D * (h % 2), D * (h % 2) + D)
                        mm = pe.matmul(B_S[h][:, at:at + w], zqk[r, g, 0, pair, t * P:(t + 1) * P], zqk[r, g, 1, pair, k0:k0 + w],
                                       start=False, stop=True, tile_position=(D * (h % 2), 0), skip_group_check=True)
                        if t == TT - 1:
                            mm.then_inc(S["qk_done"], 1)
                    at += w

            def transpose_probs(kind, n, pair):
                late = P if kind == "causal" else WIN
                for h in (2 * pair, 2 * pair + 1):
                    pe.wait_ge(S["pn_ready"], HG * n + h + 1)
                    pe.transpose(B_S[h][:, 0:P], probs[:, h, 2 * P:3 * P], ident)
                    pe.transpose(B_S[h][:, P:2 * P], probs[:, h, 0:P], ident)
                    pe.transpose(B_S[h][:, 2 * P:2 * P + late], probs[0:late, h, P:2 * P], ident[0:late, 0:late]).then_inc(S["pt_done"], 1)

            def weigh_values(kind, n, g, pair, odd):
                late = P if kind == "causal" else WIN
                if pair == 0:
                    after(pe, "yt_ready", n)
                    pe.wait_ge(S["v_ready"], n + 1)
                for h in (2 * pair, 2 * pair + 1):
                    pt_taken(n, h)
                    f = slice(g * GW + h * D, g * GW + (h + 1) * D)
                    rows, at = slice(D * (h % 2), D * (h % 2) + D), T * pair
                    pe.matmul(B_Y[rows, at:at + P + late], v_sb[:, odd, 0, f], probs_t[:, h, P:2 * P + late], start=True, stop=True,
                              tile_position=(0, D * (h % 2)), skip_group_check=True)
                    mm = pe.matmul(B_Y[rows, at + P:at + T], v_sb[:, odd, 1, f], probs_t[:, h, 0:P], start=False, stop=True,
                                   tile_position=(0, D * (h % 2)), skip_group_check=True)
                if pair == 1:
                    mm.then_inc(S["pv_done"], 1)

            def norms(n1):
                pe.wait_ge(S["v_ready"], n1 + 1)
                pe.wait_ge(S["sums_ready"], n1 + 1)
                pe.matmul(B_N[:, :], con("blk"), sqs[:, :, :].rearrange("p a t -> p (a t)"), start=True, stop=True).then_inc(S["n_done"], 1)

            def values(kind, n1, g):
                if kind == "causal":
                    after(pe, "v_ready", n1)
                else:
                    pe.wait_ge(S["ln_done"], n1)
                cols = slice(g * GW, (g + 1) * GW)
                for t in range(TT):
                    dst, tokens = B_N[:, t * GW:(t + 1) * GW], slice(t * P, (t + 1) * P)
                    if kind == "causal":
                        mm = pe.matmul(dst, latent[:, tokens], wv[:, cols], start=True, stop=True)
                    else:
                        pe.matmul(dst, x_high[:, tokens], w_high[:, 2, cols], start=True, stop=False)
                        pe.matmul(dst, x_high[:, tokens], w_low[:, 2, cols], start=False, stop=False)
                        mm = pe.matmul(dst, x_low[:, tokens], w_high[:, 2, cols], start=False, stop=True)
                mm.then_inc(S["v_done"], 1)

            def q_taken(kind, n):
                if kind == "causal":
                    after(pe, "zq_ready", n)
                else:
                    pe.wait_ge(S["q_prod"], n)
                    pe.wait_ge(S["q_square"], n)

            def k_taken(kind, n):
                if kind == "causal":
                    after(pe, "zk_ready", n)
                else:
                    pe.wait_ge(S["k_prod"], n)
                    pe.wait_ge(S["k_square"], n)

            def project(kind, k, bankx, g, src, mark):
                for half in range(2):
                    cols, dst = slice(g * GW + half * P, g * GW + half * P + P), bankx[:, half * T:(half + 1) * T]
                    if kind == "causal":
                        mm = pe.matmul(dst, w_qkv[:, k, cols], src, start=True, stop=True)
                    else:
                        pe.matmul(dst, w_high[:, k, cols], x_high[:, :], start=True, stop=False)
                        pe.matmul(dst, w_low[:, k, cols], x_high[:, :], start=False, stop=False)
                        mm = pe.matmul(dst, w_high[:, k, cols], x_low[:, :], start=False, stop=True)
                mm.then_inc(S[mark], 1)

            def output_projection(ph, i, dst):
                pe.wait_ge(S["wo_in"], 16 * (ph + 1))
                pe.wait_ge(S["yt_ready"], G * i)
                for c in range(HD // P):
                    m = pe.matmul(dst[:, 0:T], wo[:, c, :], yt[:, c, :], start=(c == 0), stop=(c == HD // P - 1))
                m.then_inc(S["wo_done"], 1)

            def up_chunk(m, b, ph, banks, c):
                if c == 0:
                    pe.wait_ge(S["w1_in"], 16 * ph)
                    pe.wait_ge(S["xh_ready"], m + 1)
                pe.wait_ge(S["hid_ready"], 3 * m if banks is TURN_BANKS else 3 * m + c - 1)
                for k, at in ((0, 0), (1, INNER)):
                    mm = pe.matmul(banks[c][0:CW[c], k * T:(k + 1) * T], w1[:, at + c * P:at + c * P + CW[c]], xh[:, b, :], start=True, stop=True)
                mm.then_inc(S["up_done"], 1)

            def up(m, b, ph, banks):
                for c in range(3):
                    up_chunk(m, b, ph, banks, c)

            def down(m, ph, out_bank):
                pe.wait_ge(S["w2_in"], 32 * ph)
                pe.wait_ge(S["mlp_res"], m)
                pe.wait_ge(S["hid_ready"], 3 * m + 3)
                for c in range(3):
                    mm = pe.matmul(out_bank[:, 0:T], w2[0:CW[c], c, :], hid[0:CW[c], c, :], start=(c == 0), stop=(c == 2))
                mm.then_inc(S["mlp_done"], 1)

            def post_taken(kind, i, g):
                if g == 1:
                    pe.wait_ge(S["res_done"], i)
                if kind == "local" and g == 2:
                    pe.wait_ge(S["xc_ready"], i)
                if kind == "local" and g == 3:
                    pe.wait_ge(S["ln_var"], i)

            def step(kind, ph, b, has, g, odd):
                i = ph * NB + b
                s1, s2, post = ("s1" in has), ("s2" in has), ("post" in has)
                n, n1 = i * G + g, stage1_batch(i, has) * G + g
                mlp, m, late = "mlp" in has, ph * NB, late_pair(g, has)
                s1_ph, n1_batch = ph + 1 if "turn" in has else ph, stage1_batch(i, has)
                begun, whole = (BEGUN[g], WHOLE[g]) if mlp and s2 else (None, None)
                if s2:
                    scores(kind, i, g, 0)
                if late:
                    transpose_probs(kind, n - 1, 1)
                if s2 and kind == "local" and norms_due(g, has):
                    norms(n1 - 1)
                if mlp and s2:
                    if g == 0:
                        q_taken("local", n1)
                    else:
                        pe.wait_ge(S["mlp_res"], m + WHOLE[g - 1] + 1)
                if post and g and "turn" not in has:
                    q_taken(kind, n1 if s1 else i * G + G if s2 else i * G)
                if post and g == 1:
                    output_projection(ph, i, post_bank(has))
                if post and kind == "local" and g == 2:
                    pe.wait_ge(S["res_done"], i)
                    pe.matmul(post_bank(has)[:, 0:T], con("center"), xs[:, ds(b - 1, 1), 0:T].rearrange("p a t -> p (a t)"), start=True, stop=True).then_inc(S["xc_done"], 1)
                if post and kind == "local" and g == 3:
                    pe.wait_ge(S["xc_squared"], i)
                    pe.matmul(post_bank(has)[:, 0:T], con("avg"), xc2[:, :], start=True, stop=True).then_inc(S["var_done"], 1)
                if s1:
                    if g == 0:
                        if kind == "local":
                            pe.wait_ge(S["xin_ready"], n1_batch + 1)
                        if kind == "causal":
                            pe.wait_ge(S["wqk_in"], 32)
                            pe.wait_ge(S["wv_in"], 16)
                        else:
                            pe.wait_ge(S["w_split"], s1_ph)
                        if "turn" in has:
                            pe.wait_ge(S["hid_ready"], 3 * (m + NB - 2))
                            pe.wait_ge(S["mlp_res"], m + NB - 2)
                    k_taken(kind, n1)
                    project(kind, 1, B_K, g, xh[:, ds(b + 1, 1), :].rearrange("p a t -> p (a t)") if kind == "causal" else None, "k_done")
                if late:
                    weigh_values(kind, n - 1, (g - 1) % G, 1, odd if g else 1 - odd)
                if mlp and not s2 and g == 0:
                    for h in range(HG):
                        pt_taken(n - 1, h)
                    up(m + NB - 2, NB - 2, ph, TURN_BANKS)
                if mlp and s2:
                    post_taken(kind, i, g)
                if begun is not None:
                    down(m + begun, ph, B_Q)
                if s2:
                    scores(kind, i, g, 1)
                    transpose_probs(kind, n, 0)
                if s1:
                    q_taken(kind, n1)
                    if post and "turn" not in has:
                        post_taken(kind, i, g)
                    project(kind, 0, B_Q, g, attn[:, ds(b + 1, 1), :].rearrange("p a t -> p (a t)") if kind == "causal" else None, "q_done")
                if not s2 and kind == "local" and norms_due(g, has):
                    norms(n1 - 1)
                if mlp and s2 and g == 0:
                    k_taken("local", n1)
                    pe.wait_ge(S["ln_done"], n1)
                if whole is not None:
                    for c in range(2):
                        up_chunk(m + whole, whole, ph, late_banks(whole), c)
                if s1:
                    if kind == "causal" and g == 0:
                        pe.wait_ge(S["xin_ready"], n1_batch + 1)
                    values(kind, n1, g)
                if s2:
                    weigh_values(kind, n, g, 0, odd)
                if whole is not None:
                    up_chunk(m + whole, whole, ph, late_banks(whole), 2)
                    up_chunk(m + BEGUN[g + 1], BEGUN[g + 1], ph, late_banks(BEGUN[g + 1]), 0)
                    down(m + whole, ph, B_Q)
                    for c in (1, 2):
                        up_chunk(m + BEGUN[g + 1], BEGUN[g + 1], ph, late_banks(BEGUN[g + 1]), c)
                if mlp and not s2 and g == 0:
                    pe.wait_ge(S["yt_ready"], i * G)
                    down(m + NB - 2, ph, B_Y)
                if mlp and not s2 and g == G - 1:
                    up(m + NB - 1, NB - 1, ph, TURN_BANKS)
                    down(m + NB - 1, ph, B_Y)

            causal = lambda ph, b, has, g, odd: step("causal", ph, b, has, g, odd)
            local = lambda ph, b, has, g, odd: step("local", ph, b, has, g, odd)
            first_batch(causal, 0)
            middle(pe, causal, 0)
            last_batch(causal, 0)
            turn(causal, 0, ("post",))
            pe.wait_ge(S["probs_zero"], 1)
            pe.wait_ge(S["zq_ready"], STEPS)
            pe.wait_ge(S["zk_ready"], STEPS)
            pe.wait_ge(S["res_done"], NB)
            credit(pe, per_step="n_done", per_batch="xc_done var_done mlp_done", per_chunk="up_done")
            first_batch(local, 1)

            def start(l):
                pe.wait_ge(S["hid_ready"], 3 * NB * (l + 1))
                pe.wait_ge(S["mlp_res"], NB * (l + 1))

            layers(pe, local, start=start)
            for p in range(PAIRS):
                pe.wait_ge(S["fin_sum"], p + 1)
                for k in range(2 * TT):
                    m = pe.transpose(bank[p][:, k * P:(k + 1) * P], xh[:, 2 * p + k // 2, (k % 2) * P:(k % 2 + 1) * P], ident)
                m.then_inc(S["fin_done"], 1)

        @block.vector
        def _(dve):
            dve.wait_ge(S["const_in"], 16)
            dve.tensor_copy(ident_b[:, :], ident).then_inc(S["masks_ready"], 1)
            dve.tensor_copy(mask_b["causal"][:, :], con("mask_causal")).then_inc(S["masks_ready"], 1)
            dve.tensor_copy(mask_b["local"][:, :], con("mask_local")).then_inc(S["masks_ready"], 1)
            NT = NB * TT
            dve.wait_ge(S["x_in"], 16)
            dve.tensor_reduce(stats[:, 0, :], x_rows[:, :, :], AX_X, ALU.add).then_inc(S["mean"], 1)
            dve.wait_ge(S["mean"], 1)
            dve.tensor_scalar(stats[:, 1, :], stats[:, 0, :], 1.0 / P, None, ALU.mult).then_inc(S["mean"], 1)
            dve.wait_ge(S["mean"], 2)
            dve.tensor_tensor(xn_rows[:, :, :], x_rows[:, :, :], stats[:, 1, :].unsqueeze(2).broadcast_to([P, NT, P]), ALU.subtract).then_inc(S["centred"], 1)
            dve.wait_ge(S["squared"], 1)
            dve.tensor_reduce(stats[:, 1, :], xh[:, :, :].rearrange("p a (t c) -> p (a t) c", c=P), AX_X, ALU.add).then_inc(S["var_sum"], 1)
            dve.wait_ge(S["rstd_row"], 1)
            dve.tensor_tensor(xn_rows[:, :, :], xn_rows[:, :, :], stats[:, 3, :].unsqueeze(2).broadcast_to([P, NT, P]), ALU.mult).then_inc(S["xn_ready"], 1)
            dve.wait_ge(S["zeros_ready"], 2)
            for p in range(PAIRS):
                dve.wait_ge(S["xnt_done"], p + 1)
                src = bank[p][:, :].rearrange("p (a t) -> p a t", a=2)
                dve.tensor_copy(attn[:, 2 * p:2 * p + 2, :], src).then_inc(S["xt_ready"], 1)
                dve.tensor_copy(xs[0:64, 2 * p:2 * p + 2, 0:T], src[0:64]).then_inc(S["xs_ready"], 1)
                dve.tensor_copy(xs[64:P, 2 * p:2 * p + 2, 1:T + 1], src[64:P]).then_inc(S["xs_ready"], 1)

            dve.wait_ge(S["pars_turned"], 1)
            dve.tensor_copy(pars[:, :, :], B_Q[:, 0:NPAR * DEPTH].rearrange("p (j l) -> p j l", j=NPAR)).then_inc(S["pars_ready"], 1)

            def maxima(kind, n, pair):
                for h in (2 * pair, 2 * pair + 1):
                    dve.wait_ge(S["qk_done"], HG * n + h + 1)
                    at = 0
                    for t, (k0, w) in enumerate(SPANS[kind]):
                        m = dve.tensor_reduce(nm[:, h, t:t + 1], B_S[h][:, at:at + w], AX_X, ALU.max, negate=True)
                        at += w
                    m.then_inc(S["nm_ready"], 1)

            def probabilities(kind, n, pair):
                heads = slice(2 * pair, 2 * pair + 2)
                dve.wait_ge(S["exp_done"], HG * n + 2 * pair + 2)
                dve.reciprocal(rrec[:, heads, :], rsum[:, heads, :]).then_inc(S["rrec_ready"], 1)
                dve.wait_ge(S["rrec_ready"], 2 * n + pair + 1)
                for h in (2 * pair, 2 * pair + 1):
                    for t, (k0, w) in enumerate(SPANS[kind]):
                        seen = probs[:, h, t * P + k0:t * P + k0 + w]
                        m = dve.tensor_scalar(seen, seen, rrec[:, h, t:t + 1], None, ALU.mult)
                    m.then_inc(S["pn_ready"], 1)

            def pt_out(kind, n, pair):
                for h in PT_ON_DVE:
                    if h // 2 == pair:
                        dve.wait_ge(S["pt_done"], HG * n + h + 1)
                        after(dve, "pv_done", n)
                        dve.tensor_copy(probs_t[:, h, 0:PT_COLS[kind]], B_S[h][:, 0:PT_COLS[kind]]).then_inc(S["pt_dve"], 1)

            def bound_inverse(n1):
                dve.wait_ge(S["rinv_ready"], n1 + 1)
                dve.tensor_scalar(rinv[:, :, :], rinv[:, :, :], 1e12 / ROOT, None, ALU.min).then_inc(S["inv_norm_ready"], 1)

            def normalise(j, g):
                n1 = j * G + g
                dve.wait_ge(S["rinv_ready"], n1 + 1)
                after(dve, f"z_in{(g - 2) % G}", z_landed(j - NB + (1 if g >= 2 else 0)))
                for idx, summed, mark in ((1, "k_summed", "inv_norm_ready"), (0, "q_summed", "zn_ready")):
                    dve.wait_ge(S[summed], n1 + 1)
                    dve.scalar_tensor_tensor(out=z_norm[:, g % 2, idx, :, :], in0=rinv[:, idx, :].unsqueeze(1).broadcast_to([P, 2, T]),
                                             scalar=1e12 / ROOT, in1=z_raw[:, idx, :, :], op0=ALU.min, op1=ALU.mult).then_inc(S[mark], 1)

            def rotate(n1, idx):
                squared, bankx, mark, taken = (("q_square", B_Q, "q_prod", "q_summed"), ("k_square", B_K, "k_prod", "k_summed"))[idx]
                dve.wait_ge(S[squared], n1 + 1)
                dve.wait_ge(S[taken], n1)
                src = bankx[:, :].rearrange("p (a t) -> p a t", a=2)
                dve.tensor_tensor(rot_u[:, idx, :, :], src, tabs[:, 2 * idx, :, :], ALU.mult)
                dve.tensor_tensor(rot_v[:, idx, :, :], src, tabs[:, 2 * idx + 1, :, :], ALU.mult).then_inc(S[mark], 1)

            def hidden(m, banks):
                for c in range(3):
                    dve.wait_ge(S["gelu_done"], 3 * m + c + 1)
                    dve.wait_ge(S["mlp_done"], m)
                    dve.scalar_tensor_tensor(out=hid[0:CW[c], c, :], in0=banks[c][0:CW[c], 0:T], scalar=par[0:CW[c], BA - LG + c:BA - LG + c + 1],
                                             in1=gate[0:CW[c], c, :], op0=ALU.add, op1=ALU.mult).then_inc(S["hid_ready"], 1)

            def residual(m, b, out_bank):
                dve.wait_ge(S["mlp_done"], m + 1)
                for rows, at in ((slice(0, 64), 0), (slice(64, P), 1)):
                    dst = xs[rows, b, at:at + T]
                    a = dve.scalar_tensor_tensor(out=dst, in0=out_bank[rows, 0:T], scalar=par[rows, B2 - LG:B2 - LG + 1], in1=dst, op0=ALU.add, op1=ALU.add)
                a.then_inc(S["mlp_res"], 1)

            def step(kind, ph, b, has, g, odd):
                i = ph * NB + b
                s1, s2, post = ("s1" in has), ("s2" in has), ("post" in has)
                batch = stage1_batch(i, has)
                n, n1 = i * G + g, stage1_batch(i, has) * G + g
                mlp, m = "mlp" in has, ph * NB
                if s1 and g == 0:
                    after(dve, "v_done", batch * G)
                    if kind == "causal":
                        dve.tensor_copy(latent[:, :], xh[:, ds(b + 1, 1), :].rearrange("p a t -> p (a t)")).then_inc(S["xin_ready"], 1)
                    else:
                        src = xs[:, ds(0 if "turn" in has else b + 1, 1), 0:T].rearrange("p a t -> p (a t)")
                        dve.tensor_copy(x_high[:, :], src).then_inc(S["x_high_ready"], 1)
                        dve.wait_ge(S["x_high_ready"], batch + 1)
                        dve.tensor_tensor(x_low[:, :], src, x_high[:, :].bitcast(F32), ALU.subtract).then_inc(S["xin_ready"], 1)
                late = late_pair(g, has)
                if s2:
                    maxima(kind, n, 0)
                if late:
                    pt_out(kind, n - 1, 1)
                begun, whole = (BEGUN[g], WHOLE[g]) if mlp and s2 else (None, None)
                if post and g == 1:
                    dve.wait_ge(S["wo_done"], i + 1)
                    if kind == "causal":
                        dve.tensor_copy(attn[:, ds(b - 1, 1), :].rearrange("p a t -> p (a t)"), post_bank(has)[:, 0:T]).then_inc(S["res_done"], 1)
                    else:
                        lo = xs[0:64, ds(b - 1, 1), 0:T].rearrange("p a t -> p (a t)")
                        hi = xs[64:P, ds(b - 1, 1), 1:T + 1].rearrange("p a t -> p (a t)")
                        dve.tensor_tensor(lo, post_bank(has)[0:64, 0:T], lo, ALU.add)
                        dve.tensor_tensor(hi, post_bank(has)[64:P, 0:T], hi, ALU.add).then_inc(S["res_done"], 1)
                if post and kind == "local" and g == 2:
                    dve.wait_ge(S["xc_done"], i)
                    after(dve, "xh_ready", i - 1)
                    dve.tensor_copy(xc[:, :], post_bank(has)[:, 0:T]).then_inc(S["xc_ready"], 1)
                if mlp and not s2 and g == 0:
                    hidden(m + NB - 2, TURN_BANKS)
                if begun is not None:
                    residual(m + begun, begun, B_Q)
                if s2:
                    probabilities(kind, n, 0)
                    maxima(kind, n, 1)
                    pt_out(kind, n, 0)
                if s1 and kind == "causal":
                    dve.wait_ge(S["k_done"], n1 + 1)
                    after(dve, "qk_done", HG * (n1 + 1 - G))
                    dve.tensor_copy(zqk[:, g, 1, :, :], B_K[:, :].rearrange("p (a t) -> p a t", a=2)).then_inc(S["zk_ready"], 1)
                if s2 and kind == "local" and norms_due(g, has):
                    bound_inverse(n1 - 1)
                if s1 and kind == "local":
                    rotate(n1, 1)
                if post and kind == "local" and g == 3:
                    dve.wait_ge(S["rstd_ready"], i)
                    dve.tensor_tensor(xc[:, :], xc[:, :], rstd[:, :], ALU.mult).then_inc(S["xh_raw"], 1)
                if s2:
                    probabilities(kind, n, 1)
                if whole is not None:
                    hidden(m + whole, late_banks(whole))
                    residual(m + whole, whole, B_Q)
                    hidden(m + BEGUN[g + 1], late_banks(BEGUN[g + 1]))
                if s1 and kind == "local":
                    rotate(n1, 0)
                if not s2 and kind == "local" and norms_due(g, has):
                    normalise(batch if g else batch - 1, (g - 1) % G)
                if mlp and not s2 and g == 0:
                    residual(m + NB - 2, NB - 2, B_Y)
                if mlp and not s2 and g == G - 1:
                    hidden(m + NB - 1, TURN_BANKS)
                    residual(m + NB - 1, NB - 1, B_Y)

            def rotary_tables(l):
                dve.wait_ge(S["q_prod"], (l + 1) * STEPS)
                dve.wait_ge(S["k_prod"], (l + 1) * STEPS)
                after(dve, "tabs_ready", l)
                dve.tensor_copy(par_rot[:, :], pars[:, 0:LG, ds(l, 1)].rearrange("p n a -> p (n a)")).then_inc(S["par_rot_ready"], 1)
                dve.wait_ge(S["par_rot_ready"], l + 1)
                for k, (c1, sign) in enumerate(((Q1, 1), (Q1, -1), (K1, 1), (K1, -1))):
                    for half in range(2):
                        m = dve.tensor_scalar(tabs[:, k, half, :], con("rot")[:, k * T:(k + 1) * T], par_rot[:, c1 + half:c1 + half + 1],
                                              float(sign if half else 1), ALU.mult, ALU.mult)
                m.then_inc(S["tabs_ready"], 1)
                dve.wait_ge(S["tabs_ready"], l + 1)

            def start(l):
                dve.wait_ge(S["mlp_res"], (l + 1) * NB)
                dve.wait_ge(S["gelu_done"], 3 * (l + 1) * NB)
                dve.tensor_copy(par[:, :], pars[:, LG:NPAR, ds(l, 1)].rearrange("p n a -> p (n a)")).then_inc(S["par_ready"], 1)
                dve.wait_ge(S["par_ready"], l + 1)

            causal = lambda ph, b, has, g, odd: step("causal", ph, b, has, g, odd)
            local = lambda ph, b, has, g, odd: step("local", ph, b, has, g, odd)
            dve.wait_ge(S["latent_ready"], PAIRS)
            first_batch(causal, 0)
            middle(dve, causal, 0)
            last_batch(causal, 0)
            turn(causal, 0, ("post",))
            credit(dve, per_step="q_prod k_prod inv_norm_ready", per_batch="x_high_ready xc_ready xh_raw mlp_res", per_chunk="hid_ready")
            rotary_tables(0)
            first_batch(local, 1)
            layers(dve, local, start=start, between=lambda l: rotary_tables(l + 1))
            dve.wait_ge(S["mlp_res"], (DEPTH + 1) * NB)
            dve.wait_ge(S["x_in"], 32)
            for p in range(PAIRS):
                for rows, at in ((slice(0, 64), 0), (slice(64, P), 1)):
                    a = dve.tensor_tensor(xh[rows, 2 * p:2 * p + 2, :], xs[rows, 2 * p:2 * p + 2, at:at + T], attn[rows, 2 * p:2 * p + 2, :], ALU.add)
                a.then_inc(S["fin_sum"], 1)
            for p in range(PAIRS):
                dve.wait_ge(S["fin_done"], p + 1)
                tiles = slice(2 * TT * p, 2 * TT * (p + 1))
                dve.tensor_tensor(xn_rows[:, tiles, :], bank[p][:, :].rearrange("p (k c) -> p k c", c=P), x_rows[:, tiles, :], ALU.add).then_inc(S["rows_ready"], 1)


_INS = ["L0_attn_x", "L0_attn_w_kv_down", "L0_attn_w_kv_up", "L0_attn_w_q", "L0_attn_w_out", "L0_ffn_Wqkv",
        "L0_ffn_q_scale", "L0_ffn_k_scale", "L0_ffn_Wo", "L0_ffn_ln_g", "L0_ffn_ln_b", "L0_ffn_W1", "L0_ffn_b1",
        "L0_ffn_W2", "L0_ffn_b2"]


def kernel(**inputs):
    import concourse.bacc as bacc
    from concourse.bass_utils import run_bass_kernel_spmd

    nc = bacc.Bacc("TRN2", target_bir_lowering=False, num_devices=1)
    arrays = {f"in_{name}": np.ascontiguousarray(inputs[name]) for name in _INS}
    arrays["in_constants"] = constants()
    for name, ranges in (("L0_ffn_Wqkv", 2),):
        a = arrays[f"in_{name}"].copy()
        for k in range(ranges):
            part = a[..., k * HD:(k + 1) * HD].reshape(*a.shape[:-1], G, HG, 2, D // 2)
            a[..., k * HD:(k + 1) * HD] = np.moveaxis(part, -2, -3).reshape(*a.shape[:-1], HD)
        arrays[f"in_{name}"] = a
    args = [nc.dram_tensor(n, a.shape, F32, kind="ExternalInput").ap() for n, a in arrays.items()]
    out = nc.dram_tensor("out_0", (NB, T, P), F32, kind="ExternalOutput").ap()
    build(nc, *args, out)
    r = run_bass_kernel_spmd(nc, [arrays], core_ids=[0])
    return r.results[0]["out_0"]
```
